# Optimizing a Trainium2 kernel written in Bass

```python
import numpy as np
import jax
import jax.numpy as jnp

def _softmax(x, axis=-1):
    return jax.nn.softmax(x, axis=axis)

def _gelu(x):
    return jax.nn.gelu(x, approximate=True)

def _silu(x):
    return jax.nn.silu(x)

def _sigmoid(x):
    return jax.nn.sigmoid(x)

def _layernorm(x, axis=-1, eps=1e-05):
    m = jnp.mean(x, axis=axis, keepdims=True)
    v = jnp.var(x, axis=axis, keepdims=True)
    return (x - m) / jnp.sqrt(v + eps)

def _scatter_add(tgt, idx, src, axis=0):
    return tgt.at[idx].add(src)

def _segment_sum(src, seg, n):
    return jax.ops.segment_sum(src, seg, n)
kernel_name = 'mk_metaformer_d2_conv_nhwc256_r4_8f92ba'

def setup_inputs(seed: int=0):
    np.random.seed(seed)
    _w = jnp.asarray

    def _rec_inputs():
        import jax
        import jax.numpy as jnp
        _gk = jax.random.key(seed)
        x = -0.0002928 + 1 * jax.random.normal(jax.random.fold_in(_gk, 1), (4, 16, 16, 64), jnp.float32)
        return x
    x = _rec_inputs()

    def _L0_conv_setup():
        import jax, jax.numpy as jnp
        import numpy as np
        MAX_LR = 0.1

        def _l2norm(x):
            n = jnp.linalg.norm(x, axis=-1, keepdims=True)
            return x / jnp.maximum(n, 1e-12)

        def _mlp(params, h):
            for w1, w2 in params:
                h = h + jax.nn.gelu(h @ w1) @ w2
            return h
        key = jax.random.key(seed)
        ks = jax.random.split(key, 11)
        B, T, C, D, DE = (4, 16, 16, 64, 128)
        s = 0.02
        return {'x': jax.random.normal(ks[0], (B, T, C, D), jnp.float32), 'Wq': jax.random.normal(ks[1], (D, D), jnp.float32) * s, 'Wk': jax.random.normal(ks[2], (D, D), jnp.float32) * s, 'Wv': jax.random.normal(ks[3], (D, D), jnp.float32) * s, 'w_lr': jax.random.normal(ks[4], (D,), jnp.float32) * s, 'w_forget': jax.random.normal(ks[5], (D,), jnp.float32) * s, 'w_eta': jax.random.normal(ks[6], (D,), jnp.float32) * s, 'w1_0': jax.random.normal(ks[7], (D, DE), jnp.float32) * s, 'w2_0': jax.random.normal(ks[8], (DE, D), jnp.float32) * s, 'w1_1': jax.random.normal(ks[9], (D, DE), jnp.float32) * s, 'w2_1': jax.random.normal(ks[10], (DE, D), jnp.float32) * s}
    _L0_conv_all = _L0_conv_setup()
    _L0_conv_in = {k: v for k, v in _L0_conv_all.items() if k in ('Wq', 'Wk', 'Wv', 'w_lr', 'w_forget', 'w_eta', 'w1_0', 'w2_0', 'w1_1', 'w2_1')}
    del _L0_conv_all

    def _L0_ffn_setup():
        import jax, jax.numpy as jnp
        import numpy as np
        TOP_K = 2
        LN_EPS = 1e-05
        key = jax.random.key(seed)
        ks = jax.random.split(key, 8)
        B, S, D, E, H = (16, 256, 64, 8, 256)
        x = jax.random.normal(ks[0], (B, S, D), dtype=jnp.float32)
        Wr = jax.random.normal(ks[1], (D, E), dtype=jnp.float32) * 0.1
        br = jnp.zeros((E,), dtype=jnp.float32)
        ln_g = jnp.ones((E, D), dtype=jnp.float32)
        ln_b = jnp.zeros((E, D), dtype=jnp.float32)
        W1 = jax.random.normal(ks[2], (E, D, H), dtype=jnp.float32) * (1.0 / np.sqrt(D))
        b1 = jnp.zeros((E, H), dtype=jnp.float32)
        W2 = jax.random.normal(ks[3], (E, H, D), dtype=jnp.float32) * (1.0 / np.sqrt(H))
        b2 = jnp.zeros((E, D), dtype=jnp.float32)
        return {'x': x, 'Wr': Wr, 'br': br, 'ln_g': ln_g, 'ln_b': ln_b, 'W1': W1, 'b1': b1, 'W2': W2, 'b2': b2}
    _L0_ffn_all = _L0_ffn_setup()
    _L0_ffn_in = {k: v for k, v in _L0_ffn_all.items() if k in ('Wr', 'br', 'ln_g', 'ln_b', 'W1', 'b1', 'W2', 'b2')}
    del _L0_ffn_all

    def _L1_conv_setup():
        import jax, jax.numpy as jnp
        import numpy as np
        from jax import lax
        EXPAND = 16
        CHANNELS = 64

        def _conv(A, W, padding):
            return lax.conv_general_dilated(A, W, (1, 1), padding, dimension_numbers=('NHWC', 'HWIO', 'NHWC'))
        key = jax.random.key(seed)
        ks = jax.random.split(key, 7)
        x = jax.random.normal(ks[0], (16, 16, 16, 64), dtype=jnp.float32)
        s = 0.05
        w1 = jax.random.normal(ks[1], (1, 1, CHANNELS, EXPAND), dtype=jnp.float32) * s
        b1 = jax.random.normal(ks[2], (1, 1, 1, EXPAND), dtype=jnp.float32) * s
        w2 = jax.random.normal(ks[3], (3, 3, CHANNELS, EXPAND), dtype=jnp.float32) * s
        b2 = jax.random.normal(ks[4], (1, 1, 1, EXPAND), dtype=jnp.float32) * s
        w3 = jax.random.normal(ks[5], (1, 1, CHANNELS, 1), dtype=jnp.float32) * s
        b3 = jax.random.normal(ks[6], (1, 1, 1, 1), dtype=jnp.float32) * s
        return {'x': x, 'w1': w1, 'b1': b1, 'w2': w2, 'b2': b2, 'w3': w3, 'b3': b3}
    _L1_conv_all = _L1_conv_setup()
    _L1_conv_in = {k: v for k, v in _L1_conv_all.items() if k in ('w1', 'b1', 'w2', 'b2', 'w3', 'b3')}
    del _L1_conv_all

    def _L1_ffn_setup():
        import jax, jax.numpy as jnp
        import numpy as np
        from jax import lax
        key = jax.random.key(seed)
        B, T, I, H = (16, 512, 64, 64)
        ks = jax.random.split(key, 13)
        s = 1.0 / np.sqrt(H)

        def w(k, shape):
            return jax.random.uniform(k, shape, jnp.float32, -s, s)
        return {'x': jax.random.normal(ks[0], (B, T, I), jnp.float32), 'U_i': w(ks[1], (I, H)), 'V_i': w(ks[2], (H, H)), 'b_i': w(ks[3], (H,)), 'U_f': w(ks[4], (I, H)), 'V_f': w(ks[5], (H, H)), 'b_f': w(ks[6], (H,)), 'U_c': w(ks[7], (I, H)), 'V_c': w(ks[8], (H, H)), 'b_c': w(ks[9], (H,)), 'U_o': w(ks[10], (I, H)), 'V_o': w(ks[11], (H, H)), 'b_o': w(ks[12], (H,))}
    _L1_ffn_all = _L1_ffn_setup()
    _L1_ffn_in = {k: v for k, v in _L1_ffn_all.items() if k in ('U_i', 'V_i', 'b_i', 'U_f', 'V_f', 'b_f', 'U_c', 'V_c', 'b_c', 'U_o', 'V_o', 'b_o')}
    del _L1_ffn_all
    return {'x': x, 'L0_conv_Wq': _L0_conv_in['Wq'], 'L0_conv_Wk': _L0_conv_in['Wk'], 'L0_conv_Wv': _L0_conv_in['Wv'], 'L0_conv_w_lr': _L0_conv_in['w_lr'], 'L0_conv_w_forget': _L0_conv_in['w_forget'], 'L0_conv_w_eta': _L0_conv_in['w_eta'], 'L0_conv_w1_0': _L0_conv_in['w1_0'], 'L0_conv_w2_0': _L0_conv_in['w2_0'], 'L0_conv_w1_1': _L0_conv_in['w1_1'], 'L0_conv_w2_1': _L0_conv_in['w2_1'], 'L0_ffn_Wr': _L0_ffn_in['Wr'], 'L0_ffn_br': _L0_ffn_in['br'], 'L0_ffn_ln_g': _L0_ffn_in['ln_g'], 'L0_ffn_ln_b': _L0_ffn_in['ln_b'], 'L0_ffn_W1': _L0_ffn_in['W1'], 'L0_ffn_b1': _L0_ffn_in['b1'], 'L0_ffn_W2': _L0_ffn_in['W2'], 'L0_ffn_b2': _L0_ffn_in['b2'], 'L1_conv_w1': _L1_conv_in['w1'], 'L1_conv_b1': _L1_conv_in['b1'], 'L1_conv_w2': _L1_conv_in['w2'], 'L1_conv_b2': _L1_conv_in['b2'], 'L1_conv_w3': _L1_conv_in['w3'], 'L1_conv_b3': _L1_conv_in['b3'], 'L1_ffn_U_i': _L1_ffn_in['U_i'], 'L1_ffn_V_i': _L1_ffn_in['V_i'], 'L1_ffn_b_i': _L1_ffn_in['b_i'], 'L1_ffn_U_f': _L1_ffn_in['U_f'], 'L1_ffn_V_f': _L1_ffn_in['V_f'], 'L1_ffn_b_f': _L1_ffn_in['b_f'], 'L1_ffn_U_c': _L1_ffn_in['U_c'], 'L1_ffn_V_c': _L1_ffn_in['V_c'], 'L1_ffn_b_c': _L1_ffn_in['b_c'], 'L1_ffn_U_o': _L1_ffn_in['U_o'], 'L1_ffn_V_o': _L1_ffn_in['V_o'], 'L1_ffn_b_o': _L1_ffn_in['b_o']}

def reference(x, L0_conv_Wq, L0_conv_Wk, L0_conv_Wv, L0_conv_w_lr, L0_conv_w_forget, L0_conv_w_eta, L0_conv_w1_0, L0_conv_w2_0, L0_conv_w1_1, L0_conv_w2_1, L0_ffn_Wr, L0_ffn_br, L0_ffn_ln_g, L0_ffn_ln_b, L0_ffn_W1, L0_ffn_b1, L0_ffn_W2, L0_ffn_b2, L1_conv_w1, L1_conv_b1, L1_conv_w2, L1_conv_b2, L1_conv_w3, L1_conv_b3, L1_ffn_U_i, L1_ffn_V_i, L1_ffn_b_i, L1_ffn_U_f, L1_ffn_V_f, L1_ffn_b_f, L1_ffn_U_c, L1_ffn_V_c, L1_ffn_b_c, L1_ffn_U_o, L1_ffn_V_o, L1_ffn_b_o):
    import jax
    import jax.numpy as jnp

    def _L0_conv_ref(x, Wq, Wk, Wv, w_lr, w_forget, w_eta, w1_0, w2_0, w1_1, w2_1):
        import jax, jax.numpy as jnp
        import numpy as np
        MAX_LR = 0.1

        def _l2norm(x):
            n = jnp.linalg.norm(x, axis=-1, keepdims=True)
            return x / jnp.maximum(n, 1e-12)

        def _mlp(params, h):
            for w1, w2 in params:
                h = h + jax.nn.gelu(h @ w1) @ w2
            return h
        B = x.shape[0]
        mem0 = ((w1_0, w2_0), (w1_1, w2_1))
        params0 = jax.tree.map(lambda p: jnp.broadcast_to(p, (B,) + p.shape), mem0)
        mom0 = jax.tree.map(jnp.zeros_like, params0)
        q = _l2norm(jnp.einsum('btcd,de->btce', x, Wq))

        def assoc_loss(p, k, v):
            pred = _mlp(p, k)
            return jnp.mean((pred - v) ** 2)
        grad_fn = jax.vmap(jax.grad(assoc_loss))

        def step(carry, x_t):
            params, mom = carry
            k = _l2norm(x_t @ Wk)
            v = x_t @ Wv
            lr = MAX_LR * jnp.mean(jax.nn.sigmoid(x_t @ w_lr), axis=1)
            forget = jnp.mean(jax.nn.sigmoid(x_t @ w_forget), axis=1)
            eta = jnp.mean(jax.nn.sigmoid(x_t @ w_eta), axis=1)
            g = grad_fn(params, k, v)

            def upd_m(m, gg):
                sh = (B,) + (1,) * (m.ndim - 1)
                return eta.reshape(sh) * m - lr.reshape(sh) * gg
            new_mom = jax.tree.map(upd_m, mom, g)

            def upd_p(p, nm):
                sh = (B,) + (1,) * (p.ndim - 1)
                return p * (1.0 - forget.reshape(sh)) + nm
            new_params = jax.tree.map(upd_p, params, new_mom)
            return ((new_params, new_mom), None)
        (paramsT, momT), _ = jax.lax.scan(step, (params0, mom0), jnp.swapaxes(x, 0, 1))
        final = jax.tree.map(lambda p: jnp.mean(p, axis=0), paramsT)
        return _mlp(final, q)

    def _L0_ffn_ref(x, Wr, br, ln_g, ln_b, W1, b1, W2, b2):
        import jax, jax.numpy as jnp
        import numpy as np
        TOP_K = 2
        LN_EPS = 1e-05
        B, S, D = x.shape
        N = B * S
        xt = x.reshape(N, D)
        logits = xt @ Wr + br
        probs = jax.nn.softmax(logits, axis=-1)
        top_p, top_idx = jax.lax.top_k(probs, TOP_K)
        weights = top_p / top_p.sum(axis=-1, keepdims=True)
        mu = xt.mean(axis=-1, keepdims=True)
        var = ((xt - mu) ** 2).mean(axis=-1, keepdims=True)
        xn = (xt - mu) * jax.lax.rsqrt(var + LN_EPS)
        xe = xn[None, :, :] * ln_g[:, None, :] + ln_b[:, None, :]
        h = jax.nn.gelu(jnp.einsum('end,edh->enh', xe, W1) + b1[:, None, :], approximate=False)
        y = jnp.einsum('enh,ehd->end', h, W2) + b2[:, None, :]
        y_tok = jnp.transpose(y, (1, 0, 2))
        sel = jnp.take_along_axis(y_tok, top_idx[:, :, None], axis=1)
        out = (weights[:, :, None] * sel).sum(axis=1)
        return out.reshape(B, S, D)

    def _L1_conv_ref(x, w1, b1, w2, b2, w3, b3):
        import jax, jax.numpy as jnp
        import numpy as np
        from jax import lax
        EXPAND = 16
        CHANNELS = 64

        def _conv(A, W, padding):
            return lax.conv_general_dilated(A, W, (1, 1), padding, dimension_numbers=('NHWC', 'HWIO', 'NHWC'))
        depth_batch = CHANNELS // EXPAND

        def step1(A, i):
            Z = _conv(A, w1, 'VALID') + b1
            A = lax.dynamic_update_slice(A, Z, (0, 0, 0, i * EXPAND))
            return (A, None)

        def step2(A, i):
            Z = _conv(A, w2, 'SAME') + b2
            A = lax.dynamic_update_slice(A, Z, (0, 0, 0, i * EXPAND))
            return (A, None)

        def step3(A, i):
            Z = _conv(A, w3, 'VALID') + b3
            A = lax.dynamic_update_slice(A, Z, (0, 0, 0, i))
            return (A, None)
        A = x
        A, _ = lax.scan(step1, A, jnp.arange(depth_batch))
        A = jax.nn.relu(A)
        A, _ = lax.scan(step2, A, jnp.arange(depth_batch))
        A = jax.nn.relu(A)
        A, _ = lax.scan(step3, A, jnp.arange(CHANNELS))
        return A + x

    def _L1_ffn_ref(x, U_i, V_i, b_i, U_f, V_f, b_f, U_c, V_c, b_c, U_o, V_o, b_o):
        import jax, jax.numpy as jnp
        import numpy as np
        from jax import lax
        B, T, _ = x.shape
        H = U_i.shape[1]
        xt = jnp.swapaxes(x, 0, 1)
        xi = xt @ U_i + b_i
        xf = xt @ U_f + b_f
        xg = xt @ U_c + b_c
        xo = xt @ U_o + b_o
        h0 = jnp.zeros((B, H), x.dtype)
        c0 = jnp.zeros((B, H), x.dtype)

        def step(carry, xs):
            h, c = carry
            xi_t, xf_t, xg_t, xo_t = xs
            i_t = jax.nn.sigmoid(xi_t + h @ V_i)
            f_t = jax.nn.sigmoid(xf_t + h @ V_f)
            g_t = jnp.tanh(xg_t + h @ V_c)
            o_t = jax.nn.sigmoid(xo_t + h @ V_o)
            c_new = h * c + i_t * g_t
            h_new = o_t * jnp.tanh(c_new)
            return ((h_new, c_new), h_new)
        (_, _), hs = lax.scan(step, (h0, c0), (xi, xf, xg, xo))
        return jnp.swapaxes(hs, 0, 1)

    def _gn(v, G=32, eps=1e-05):
        B_, H_, W_, C_ = v.shape
        g = v.reshape(B_, H_, W_, G, C_ // G)
        m = jnp.mean(g, axis=(1, 2, 4), keepdims=True)
        s = jnp.var(g, axis=(1, 2, 4), keepdims=True)
        return ((g - m) / jnp.sqrt(s + eps)).reshape(v.shape)

    def _ln_c(v, eps=1e-06):
        m = jnp.mean(v, axis=-1, keepdims=True)
        s = jnp.var(v, axis=-1, keepdims=True)
        return (v - m) / jnp.sqrt(s + eps)

    def _ln_t(v, eps=1e-05):
        m = jnp.mean(v, axis=-1, keepdims=True)
        s = jnp.var(v, axis=-1, keepdims=True)
        return (v - m) / jnp.sqrt(s + eps)

    def _to_tokens(v):
        B_, H_, W_, C_ = v.shape
        return v.reshape(B_, H_ * W_, C_)

    def _from_tokens(t, like):
        return t.reshape(like.shape)
    x = x + _L0_conv_ref(_ln_c(x), L0_conv_Wq, L0_conv_Wk, L0_conv_Wv, L0_conv_w_lr, L0_conv_w_forget, L0_conv_w_eta, L0_conv_w1_0, L0_conv_w2_0, L0_conv_w1_1, L0_conv_w2_1)
    t = _to_tokens(x)
    t = t + _L0_ffn_ref(_ln_t(t), L0_ffn_Wr, L0_ffn_br, L0_ffn_ln_g, L0_ffn_ln_b, L0_ffn_W1, L0_ffn_b1, L0_ffn_W2, L0_ffn_b2)
    x = _from_tokens(t, x)
    x = x + _L1_conv_ref(_ln_c(x), L1_conv_w1, L1_conv_b1, L1_conv_w2, L1_conv_b2, L1_conv_w3, L1_conv_b3)
    t = _to_tokens(x)
    t = t + _L1_ffn_ref(_ln_t(t), L1_ffn_U_i, L1_ffn_V_i, L1_ffn_b_i, L1_ffn_U_f, L1_ffn_V_f, L1_ffn_b_f, L1_ffn_U_c, L1_ffn_V_c, L1_ffn_b_c, L1_ffn_U_o, L1_ffn_V_o, L1_ffn_b_o)
    x = _from_tokens(t, x)
    return x

_drawn_inputs = setup_inputs


def setup_inputs(seed=0):
    import zlib

    import numpy as np

    out = dict(_drawn_inputs(seed))
    spreads = {'L0_ffn_br': (0.0, 0.1),
     'L0_ffn_ln_g': (1.0, 0.2),
     'L0_ffn_ln_b': (0.0, 0.1),
     'L0_ffn_b1': (0.0, 0.1),
     'L0_ffn_b2': (0.0, 0.1)}
    factors = {'L1_conv_b1': 8.0,
     'L1_conv_b2': 8.0,
     'L1_ffn_U_i': 3.961,
     'L1_ffn_V_i': 8.0,
     'L1_ffn_b_i': 8.0,
     'L1_ffn_V_c': 8.0,
     'L1_ffn_b_c': 6.709,
     'L1_ffn_U_o': 3.795,
     'L1_ffn_V_o': 8.0,
     'L1_ffn_b_o': 8.0}
    for name, (base, spread) in spreads.items():
        noise = np.random.default_rng([zlib.crc32(name.encode()), seed]).standard_normal(out[name].shape)
        drawn = base * np.exp(spread * noise) if base else spread * noise
        out[name] = jnp.asarray(drawn.astype(out[name].dtype))
    for name, factor in factors.items():
        out[name] = (out[name] * factor).astype(out[name].dtype)
    return out
```

```python
from contextlib import ExitStack

import concourse.bass as bass
from concourse import mybir
import numpy as np

F32 = mybir.dt.float32
ALU = mybir.AluOpType
ACT = mybir.ActivationFunctionType
AX = mybir.AxisListType.X

B, T, C, D = 4, 16, 16, 64
DE = 128
NTOK = B * T * C
NT = NTOK // 128
E, H, HC = 8, 256, 2
W = 16
S = W * W
PADW = W + 2
KAPPA = 0.044715
RT2PI = float(np.sqrt(2.0 / np.pi))
LSTM_UN = 32
FILL, FILL_N = 4, 512
AFTER = (10, 10)
BUSY = (12, 1, 2, 1, 2, 2, 6, 2, 3, 1, 0, 0)
MEM_UN = 4
TP = T + MEM_UN


def wide(ap, n):
    return bass.AP(ap.tensor, ap.offset, [*ap.ap, [0, n]])


def mid(ap, n):
    return bass.AP(ap.tensor, ap.offset, [ap.ap[0], [0, n], *ap.ap[1:]])


def build(nc, i_, out):
    with ExitStack() as ctx:
        def sb(name, shape):
            return ctx.enter_context(nc.sbuf_tensor(name, shape, F32))

        names = {}

        def sem(name):
            if name not in names:
                names[name] = ctx.enter_context(nc.semaphore(name))
            return names[name]

        bk = ctx.enter_context(nc.psum_tensor("bk", [128, 8, 512], F32))

        ident = sb("ident", [128, 128])
        wqkv = sb("wqkv", [D, 3 * D])
        wgate = sb("wgate", [D, 3])
        gaff = sb("gaff", [3, 2])
        gsel = sb("gsel", [3, 3, 128])
        memw = sb("memw", [128, 2 * DE])
        wr = sb("wr", [128, E])
        br = sb("br", [128, E])
        lng = sb("lng", [D, E])
        lnb = sb("lnb", [D + 1, E])
        w1 = sb("w1", [D + 1, E, H])
        w1g = sb("w1g", [128, E, H])
        w2 = sb("w2", [128, E, HC, D])
        b2 = sb("b2", [E, D])
        c1p = sb("c1p", [D + 1, 4, D + 1])
        c1last = sb("c1last", [D + 1, D + 1])
        cw = sb("cw", [128, 6, 9, 128])
        cb2 = sb("cb2", [128, 1])
        w3 = sb("w3", [128, D])
        b3 = sb("b3", [128, 1])
        lu = sb("lu", [D + 1, 3, D])
        lv = sb("lv", [D, 3, D])
        notfirst = sb("notfirst", [128, NT * E])

        xs = sb("xs", [128, NT, D])
        xc = sb("xc", [128, NT, D])
        bst = sb("bst", [128, NT, 6])
        mv = sb("mv", [128, NT, 2])
        xn = sb("xn", [128, NT, D])
        st = sb("st", [128, NT])
        rs = sb("rs", [128, NT])
        sd = sb("sd", [128, NT])
        nt = sb("nt", [128, 2 * NT])
        qkv2 = sb("qkv2", [128, NT, 2])

        xnT = sb("xnT", [D, NTOK])
        gS = sb("gS", [3, NTOK])
        gsum = sb("gsum", [3, B * T])
        glin = sb("glin", [3, B * T])
        gates = sb("gates", [128, 3, B, TP])
        lrtok = sb("lrtok", [128, TP])
        qksq = sb("qksq", [128, NT, 2 * D])
        qkr = sb("qkr", [128, NT, 2])
        KK = sb("KK", [128, NT, 2 * D])
        QV = sb("QV", [128, NT, 2 * D])
        kk = sb("kk", [128, B, TP * C])
        qq = sb("qq", [128, NTOK])
        vT = sb("vT", [128, B, TP * C])
        kcur = [sb(f"kcur{n}", [128, B, 32]) for n in range(2)]
        vcur = [sb(f"vcur{n}", [128, B, C]) for n in range(2)]
        gcur = [sb(f"gcur{n}", [128, 3, B]) for n in range(2)]
        lrcur = [sb(f"lrcur{n}", [128, 1]) for n in range(2)]
        mem = sb("mem", [128, 5 * B * 2 * DE])

        def part(base, n, k):
            return mem[:, base:base + n * k].rearrange("p (n k) -> p n k", n=n)

        WB = B * 2 * DE
        P = part(0, B, 2 * DE)
        M = part(WB, B, 2 * DE)
        Me = part(2 * WB, B, 2 * DE)
        Pf = part(3 * WB, B, 2 * DE)
        Q = part(4 * WB, B, 2 * DE)
        w21T = sb("w21T", [128, B, DE])
        w20T = sb("w20T", [128, B, DE])
        w11T = sb("w11T", [128, B, D])
        g0T = sb("g0T", [128, B, C])
        g1T = sb("g1T", [128, B, C])
        h1T = sb("h1T", [128, B, 32])
        dT = sb("dT", [128, B, 32])
        dh1T = sb("dh1T", [128, B, 32])
        da1T = sb("da1T", [128, B, C])
        hv = sb("hv", [128, B, C])
        a0q, a0u, a0y, a0t, a0x, a0s = (sb(f"a0{c}", [128, DE]) for c in "quytxs")
        a1q, a1u, a1y, a1t, a1x, a1s = (sb(f"a1{c}", [128, DE]) for c in "quytxs")
        g0tok = sb("g0tok", [128, DE])
        h1tok = sb("h1tok", [128, D])
        g1tok = sb("g1tok", [128, DE])
        dtok = sb("dtok", [128, D])
        da1tok = sb("da1tok", [128, DE])
        dh1tok = sb("dh1tok", [128, D])
        da0tok = sb("da0tok", [128, DE])
        ktok = sb("ktok", [128, D])
        FW2 = sb("FW2", [128, 2, 2 * DE])
        FW = sb("FW", [128, 2 * DE])
        g0F = KK[:, :, :].rearrange("p n c -> p (n c)")
        g1F = QV[:, :, :].rearrange("p n c -> p (n c)")
        h1F = qksq[:, :, :].rearrange("p n c -> p (n c)")

        XT = KK
        x2A = sb("x2A", [128, NTOK])
        t1T = sb("t1T", [128, NTOK])
        L = sb("L", [128, NT, E])
        L2 = sb("L2", [128, NT, E])
        eq = sb("eq", [128, NT, E])
        cum = sb("cum", [128, NT, E])
        pick1 = sb("pick1", [128, NT, E])
        pick2 = sb("pick2", [128, NT, E])
        m1 = sb("m1", [128, NT])
        m2 = sb("m2", [128, NT])
        md = sb("md", [128, NT])
        p1 = sb("p1", [128, NT])
        p2 = sb("p2", [128, NT])
        W8 = sb("W8", [128, NT, E])
        W8T = sb("W8T", [E, NTOK])
        hT = sb("hT", [128, E, HC, NTOK // 2])
        yw = [sb(f"yw{n}", [128, E, D]) for n in range(2)]
        ysum = sb("ysum", [128, NT, D])

        c1a = sb("c1a", [D + 1, D + 1])
        c1b = sb("c1b", [D + 1, D + 1])
        xcT = x2A[0:D + 1]
        img = [sb(f"img{n}", [128, PADW, PADW]) for n in range(2)]
        zim = [sb(f"zim{n}", [128, PADW, PADW]) for n in range(2)]
        rz = [sb(f"rz{n}", [128, S]) for n in range(2)]
        sc0 = sb("sc0", [128, NT, D])
        A3 = part(3 * WB, NT, D)
        prod = part(3 * WB + NT * D, NT, D)
        sc1 = part(4 * WB, NT, D)

        t3T = part(0, S + 2 * LSTM_UN, B)[0:D + 1]
        hring = sb("hring", [D + 1, LSTM_UN, B])
        hist = part((S + 2 * LSTM_UN) * B, S + LSTM_UN, B)[0:D]
        lvh = sb("lvh", [D + 1, 3, D])
        gp = sb("gp", [D, B, 3])
        og = sb("og", [D, B])
        cs = [sb(f"cs{n}", [D, B, 3]) for n in range(2)]
        warm = sb("warm", [1, 2])
        idle = ctx.enter_context(nc.sbuf_tensor("idle", [128, 128 + FILL_N], mybir.dt.bfloat16))

        def inner(t):
            return t[:, 1:1 + W, 1:1 + W]

        block = ctx.enter_context(nc.Block())

        @block.sync
        def _(sp):
            sp.dma_start(xs[:, :, :], i_["x"]).then_inc(sem("ld_x"), 16)
            for dst, key, s in ((ident[:, :], "ident", "ld_id"), (wqkv[:, :], "wqkv", "ld_a"), (wgate[:, :], "wgate", "ld_a"),
                                (gaff[:, :], "gaff", "ld_g"), (gsel[:, :, :], "gsel", "ld_g"), (memw[:, :], "memw", "ld_m"),
                                (lng[:, :], "lng", "ld_w1"), (lnb[:, :], "lnb", "ld_w1"), (w1[:, :, :], "w1", "ld_w1"),
                                (w2[:, :, :, :], "w2", "ld_w2"), (b2[:, :], "b2", "ld_w2"),
                                (wr[D:128, :], "wr", "ld_r"), (br[:, :], "br", "ld_r"), (notfirst[:, :], "notfirst", "ld_r"),
                                (c1p[:, :, :], "c1p", "ld_c1"), (c1last[:, :], "c1last", "ld_c1"),
                                (w3[:, :], "w3", "ld_3"), (b3[:, :], "b3", "ld_3"), (cb2[:, :], "cb2", "ld_3"),
                                (lu[:, :, :], "lu", "ld_l"), (lv[:, :, :], "lv", "ld_l"),
                                (cw[:, :, :, :], "cw", "ld_cw")):
                sp.dma_start(dst, i_[key]).then_inc(sem(s), 16)
            sp.wait_ge(sem("x_done"), 1)
            sp.dma_start(out, xs[:, :, :]).then_inc(sem("stored"), 16)
            sp.wait_ge(sem("stored"), 16)

        @block.gpsimd
        def _(pool):
            for t in (*kcur, h1T, dT, dh1T):
                nc.gpsimd.memset(t[:, :, :], 0.0)
            nc.gpsimd.memset(M[:, :, :], 0.0)
            nc.gpsimd.memset(idle[:, :], 0.0)
            nc.gpsimd.memset(gates[:, :, :, :], 0.0)
            nc.gpsimd.memset(lrtok[:, :], 0.0)
            nc.gpsimd.memset(kk[:, :, S:], 0.0)
            nc.gpsimd.memset(vT[:, :, S:], 0.0)
            nc.gpsimd.memset(sc0[:, :, :], 0.0)
            nc.gpsimd.memset(gp[:, :, :], 0.0)
            for t in (*img, *zim):
                nc.gpsimd.memset(t[:, :, :], 0.0)
            nc.gpsimd.memset(qq[:, :], 0.0)
            nc.gpsimd.memset(warm[:, :], 0.0).then_inc(sem("cleared"), 1)

            def prefetch(t, n):
                nc.gpsimd.tensor_copy(kcur[n][:, :, 0:C], kview(kk, t))
                nc.gpsimd.tensor_copy(vcur[n][:, :, :], kview(vT, t))
                nc.gpsimd.tensor_copy(gcur[n][:, :, :], gates[:, :, :, bass.ds(t, 1)].rearrange("p g b o -> p g (b o)"))
                nc.gpsimd.tensor_copy(lrcur[n][:, :], lrtok[:, bass.ds(t, 1)]).then_inc(sem("pre"), 1)

            def kview(tile, t, lo=0):
                return tile[lo:128, :, bass.ds(t * C, C)]

            pool.wait_ge(sem("cleared"), 1)
            pool.wait_ge(sem("gates"), 5)
            pool.wait_ge(sem("kkT"), 4)
            prefetch(0, 0)
            with nc.gpsimd.Fori(0, T, MEM_UN) as i:
                for u in range(MEM_UN):
                    t = i + u
                    n = u % 2
                    pool.wait_ge(sem("pre"), t + 1)
                    pool.wait_ge(sem("m_new"), t + 1)
                    nc.gpsimd.tensor_tensor(Me[:, :, :], M[:, :, :], wide(gcur[n][:, 0, :], 2 * DE), ALU.mult)
                    nc.gpsimd.tensor_tensor(Pf[:, :, :], P[:, :, :], wide(gcur[n][:, 1, :], 2 * DE),
                                            ALU.mult).then_inc(sem("decayed"), 1)
                    pool.wait_ge(sem("decayed"), t + 1)
                    nc.gpsimd.tensor_tensor(Q[:, :, :], Pf[:, :, :], Me[:, :, :], ALU.add).then_inc(sem("Q"), 1)
                    prefetch(t + 1, 1 - n)

            pool.wait_ge(sem("pre"), T + 1)
            nc.gpsimd.memset(h1F[0:D, :], 0.0).then_inc(sem("h1F_zeros"), 1)
            nc.gpsimd.memset(w1g[:, :, :], 0.0)
            nc.gpsimd.memset(x2A[:, :], 0.0).then_inc(sem("zeros"), 1)
            pool.wait_ge(sem("zeros"), 1)
            pool.wait_ge(sem("ld_w1"), 48)
            nc.gpsimd.tensor_tensor(w1g[0:D, :, :], w1[0:D, :, :], wide(lng[:, :], H), ALU.mult).then_inc(sem("w1g"), 1)

            HU = LSTM_UN // 2
            nc.gpsimd.memset(hring[:, :, :], 0.0).then_inc(sem("h_saved"), HU + 1)
            with nc.gpsimd.Fori(0, S, LSTM_UN) as i:
                for u in (0, HU):
                    pool.wait_ge(sem("h_new"), i + (u + HU + 1))
                    nc.gpsimd.tensor_copy(hist[:, bass.ds(i + u, HU), :], hring[0:D, u:u + HU, :]).then_inc(sem("h_saved"), HU)

        @block.tensor
        def _(pe):
            up = ident[64:128, 64:128]

            def busy(count, bank):
                for _ in range(count):
                    nc.tensor.matmul(bk[:, bank, 0:512], idle[:, 0:128], idle[:, 128:128 + 512], start=True, stop=True)

            def keep_busy(place, bank):
                for _ in range(BUSY[place]):
                    nc.tensor.matmul(bk[:, bank, 0:256], idle[:, 0:128], idle[:, 128:128 + 256], start=True, stop=True)

            pe.wait_ge(sem("cleared"), 1)
            pe.wait_ge(sem("ld_id"), 16)
            pe.wait_ge(sem("ln"), 1)
            for n in range(NT):
                ins = nc.tensor.transpose(bk[0:D, n // 4, (n % 4) * 128:(n % 4 + 1) * 128], xn[:, n, :], ident[:, :])
                if n % 4 == 3:
                    ins.then_inc(sem("xnT_ps"), 1)
            pe.wait_ge(sem("ld_a"), 32)
            pe.wait_ge(sem("xnT"), 2)
            for n in range(2):
                nc.tensor.matmul(bk[0:3, 2 + n, :], wgate[:, :], xnT[:, n * 512:(n + 1) * 512], start=True,
                                 stop=True).then_inc(sem("glog"), 1)
            for n in range(NT):
                ins = nc.tensor.matmul(bk[:, 4 + n // 2, (n % 2) * 192:(n % 2 + 1) * 192],
                                       xnT[:, n * 128:(n + 1) * 128], wqkv[:, :], start=True, stop=True)
                if n % 2 == 1:
                    ins.then_inc(sem("qkv_ps"), 1)
            pe.wait_ge(sem("KK"), 1)
            for n in range(NT):
                ins = nc.tensor.transpose(bk[:, n // 4, (n % 4) * 128:(n % 4 + 1) * 128], KK[:, n, :], ident[:, :])
            ins.then_inc(sem("kkT_ps"), 1)
            pe.wait_ge(sem("QV"), 2)
            for n in range(NT):
                ins = nc.tensor.transpose(bk[:, 4 + n // 4, (n % 4) * 128:(n % 4 + 1) * 128], QV[:, n, :], ident[:, :])
            ins.then_inc(sem("qvT_ps"), 1)
            pe.wait_ge(sem("ld_g"), 32)
            pe.wait_ge(sem("glin"), 1)
            for g in range(3):
                ins = nc.tensor.matmul(bk[:, 2, g * B * T:(g + 1) * B * T], gsel[:, g, :], glin[:, :], start=True, stop=True)
            ins.then_inc(sem("gate_ps"), 1)
            pe.wait_ge(sem("ps_clear"), 1)

            with nc.tensor.Fori(0, T, MEM_UN) as i:
                for u in range(MEM_UN):
                    t1 = i + (u + 1)
                    kc = kcur[u % 2]
                    pe.wait_ge(sem("pre"), t1)
                    keep_busy(0, 0)
                    pe.wait_ge(sem("ld_id"), 16)
                    pe.wait_ge(sem("p1_new"), t1)
                    for b in range(B):
                        ins = nc.tensor.matmul(bk[32 * b:32 * b + C, 1, 0:DE], kc[0:D, b, 0:C], P[0:D, b, 0:DE],
                                               start=True, stop=True)
                    ins.then_inc(sem("a0tok"), 1)
                    nc.tensor.transpose(bk[:, 2, 448:448 + D], kc[0:D, :, :].rearrange("p b c -> p (b c)"),
                                        ident[0:D, 0:D]).then_inc(sem("ktok_ps"), 1)
                    keep_busy(1, 0)
                    pe.wait_ge(sem("g0tok"), t1)
                    nc.tensor.transpose(bk[:, 0, 0:128], g0tok[:, :], ident[:, :]).then_inc(sem("g0T_ps"), 1)
                    for b in range(B):
                        ins = nc.tensor.transpose(bk[:, 3, 256 + b * D:256 + (b + 1) * D], P[D:128, b, 0:DE], up)
                    ins.then_inc(sem("w11T_ps"), 1)
                    pe.wait_ge(sem("g0T"), t1)
                    pe.wait_ge(sem("p2_new"), t1)
                    for b in range(B):
                        ins = nc.tensor.matmul(bk[64:128, 2, b * C:(b + 1) * C], P[:, b, DE:DE + D], g0T[:, b, :],
                                               start=True, stop=True)
                    ins.then_inc(sem("h1_ps"), 1)
                    pe.wait_ge(sem("ld_id"), 16)
                    pe.wait_ge(sem("m_new"), t1)
                    for b in range(B):
                        ins = nc.tensor.transpose(bk[0:D, 4, b * DE:(b + 1) * DE], P[:, b, DE + D:2 * DE], ident[:, :])
                    ins.then_inc(sem("w21T_ps"), 1)
                    keep_busy(3, 7)
                    pe.wait_ge(sem("ld_id"), 16)
                    pe.wait_ge(sem("w11T"), t1)
                    pe.wait_ge(sem("h1T"), t1)
                    for b in range(B):
                        ins = nc.tensor.matmul(bk[32 * b:32 * b + C, 3, 0:DE], h1T[64:128, b, 0:C], P[D:128, b, 0:DE],
                                               start=True, stop=True)
                    ins.then_inc(sem("a1tok"), 1)
                    nc.tensor.transpose(bk[:, 0, 128:128 + D], h1T[64:128, :, :].rearrange("p b c -> p (b c)"),
                                        up).then_inc(sem("h1tok_ps"), 1)
                    keep_busy(4, 7)
                    pe.wait_ge(sem("g1tok"), t1)
                    nc.tensor.transpose(bk[:, 1, 128:256], g1tok[:, :], ident[:, :]).then_inc(sem("g1T_ps"), 1)
                    for b in range(B):
                        ins = nc.tensor.transpose(bk[0:D, 6, b * DE:(b + 1) * DE], P[:, b, DE:DE + D], ident[:, :])
                    ins.then_inc(sem("w20T_ps"), 1)
                    keep_busy(5, 7)
                    pe.wait_ge(sem("g1T"), t1)
                    for b in range(B):
                        ins = nc.tensor.matmul(bk[64:128, 2, 64 + b * C:64 + (b + 1) * C], P[:, b, DE + D:2 * DE],
                                               g1T[:, b, :], start=True, stop=True)
                    ins.then_inc(sem("pred_ps"), 1)
                    keep_busy(6, 7)
                    pe.wait_ge(sem("ld_id"), 16)
                    pe.wait_ge(sem("w21T"), t1)
                    pe.wait_ge(sem("h1tok"), t1)
                    pe.wait_ge(sem("dT"), t1)
                    for b in range(B):
                        ins = nc.tensor.matmul(bk[32 * b:32 * b + C, 2, 128:128 + DE], dT[64:128, b, 0:C], w21T[64:128, b, :],
                                               start=True, stop=True)
                    ins.then_inc(sem("dg1_ps"), 1)
                    nc.tensor.transpose(bk[:, 0, 192:192 + D], dT[64:128, :, :].rearrange("p b c -> p (b c)"),
                                        up).then_inc(sem("dtok_ps"), 1)
                    keep_busy(7, 7)
                    pe.wait_ge(sem("w20T"), t1)
                    pe.wait_ge(sem("dtok"), t1)

                    def grad21(b):
                        r = slice(32 * b, 32 * b + C)
                        nc.tensor.matmul(bk[:, 4 + b, 192:256], g1tok[r, :], dtok[r, :], start=True, stop=True)

                    grad21(0)
                    pe.wait_ge(sem("da1tok"), t1)
                    nc.tensor.transpose(bk[:, 1, 256:384], da1tok[:, :], ident[:, :]).then_inc(sem("da1T_ps"), 1)
                    grad21(1)
                    grad21(2)
                    keep_busy(9, 3)
                    pe.wait_ge(sem("da1T"), t1)
                    for b in range(B):
                        ins = nc.tensor.matmul(bk[64:128, 2, 256 + b * C:256 + (b + 1) * C], w11T[:, b, :],
                                               da1T[:, b, :], start=True, stop=True)
                    ins.then_inc(sem("dh1_ps"), 1)
                    grad21(3)
                    keep_busy(10, 3)
                    pe.wait_ge(sem("ld_id"), 16)
                    pe.wait_ge(sem("w20T"), t1)
                    pe.wait_ge(sem("dh1T"), t1)
                    nc.tensor.transpose(bk[:, 0, 256:256 + D], dh1T[64:128, :, :].rearrange("p b c -> p (b c)"),
                                        up).then_inc(sem("dh1tok_ps"), 1)
                    for b in range(B):
                        ins = nc.tensor.matmul(bk[32 * b:32 * b + C, 2, 320:320 + DE], dh1T[64:128, b, 0:C],
                                               w20T[64:128, b, :], start=True, stop=True)
                    ins.then_inc(sem("dg0_ps"), 1)
                    keep_busy(8, 3)
                    pe.wait_ge(sem("dh1tok"), t1)
                    for b in range(B):
                        r = slice(32 * b, 32 * b + C)
                        nc.tensor.matmul(bk[:, 4 + b, 128:192], g0tok[r, :], dh1tok[r, :], start=True, stop=True)
                    keep_busy(11, 3)
                    pe.wait_ge(sem("da0tok"), t1)
                    for b in range(B):
                        r = slice(32 * b, 32 * b + C)
                        nc.tensor.matmul(bk[64:128, 4 + b, 0:DE], h1tok[r, :], da1tok[r, :], start=True, stop=True)
                        ins = nc.tensor.matmul(bk[0:D, 4 + b, 0:DE], ktok[r, :], da0tok[r, :], start=True, stop=True)
                    ins.then_inc(sem("grads"), 1)

            pe.wait_ge(sem("p2_new"), T + 1)
            busy(AFTER[0], 0)
            pe.wait_ge(sem("FW"), 1)
            for n in range(2):
                nc.tensor.matmul(bk[:, 2 + n, :], FW[:, 0:DE], qq[:, n * 512:(n + 1) * 512], start=True,
                                 stop=True).then_inc(sem("f_a0"), 1)
            for n in range(2):
                pe.wait_ge(sem("f_g0"), n + 1)
                nc.tensor.matmul(bk[64:128, 4 + n, :], FW[:, DE:DE + D], g0F[:, n * 512:(n + 1) * 512], start=True,
                                 stop=True).then_inc(sem("f_h1_ps"), 1)
            pe.wait_ge(sem("h1F_zeros"), 1)
            for n in range(2):
                pe.wait_ge(sem("f_h1"), n + 1)
                nc.tensor.matmul(bk[:, 6 + n, :], FW[:, 0:DE], h1F[:, n * 512:(n + 1) * 512], start=True,
                                 stop=True).then_inc(sem("f_a1"), 1)
            for n in range(NT):
                if n % 4 == 0:
                    pe.wait_ge(sem("f_g1"), n // 4 + 1)
                nc.tensor.matmul(bk[:, n // 4, (n % 4) * D:(n % 4 + 1) * D], g1F[:, n * 128:(n + 1) * 128], FW[:, DE + D:2 * DE],
                                 start=True, stop=False)
                ins = nc.tensor.matmul(bk[:, n // 4, (n % 4) * D:(n % 4 + 1) * D], h1F[:, n * 128:(n + 1) * 128], ident[:, 64:128],
                                       start=False, stop=True)
                if n % 4 == 3:
                    ins.then_inc(sem("f_y"), 1)

            pe.wait_ge(sem("ld_c1"), 32)
            nc.tensor.matmul(bk[0:D + 1, 2, 0:D + 1], c1p[:, 2, :], c1last[:, :], start=True, stop=True).then_inc(sem("c1_ps"), 1)
            pe.wait_ge(sem("ld_w1"), 48)
            for e in range(E):
                ins = nc.tensor.matmul(bk[64:65, 4 + e // 2, (e % 2) * H:(e % 2 + 1) * H], lnb[:, e:e + 1], w1[:, e, :],
                                       start=True, stop=True)
            ins.then_inc(sem("w1row_ps"), 1)
            pe.wait_ge(sem("c1"), 1)
            nc.tensor.matmul(bk[0:D + 1, 3, 0:D + 1], c1p[:, 1, :], c1a[:, :], start=True, stop=True).then_inc(sem("c1_ps"), 1)
            pe.wait_ge(sem("c1"), 2)
            nc.tensor.matmul(bk[0:D + 1, 2, 0:D + 1], c1p[:, 0, :], c1b[:, :], start=True, stop=True).then_inc(sem("c1_ps"), 1)
            pe.wait_ge(sem("c1"), 3)
            busy(AFTER[1], 7)

            pe.wait_ge(sem("XT"), 1)
            for n in range(NT):
                ins = nc.tensor.transpose(bk[:, 2 + n // 4, (n % 4) * 128:(n % 4 + 1) * 128], XT[:, n, :], ident[:, :])
                if n % 4 == 3:
                    ins.then_inc(sem("XT_ps"), 1)
            pe.wait_ge(sem("ld_r"), 48)
            pe.wait_ge(sem("t1T"), 2)
            for n in range(NT):
                ins = nc.tensor.matmul(bk[:, 0, n * E:(n + 1) * E], t1T[64:128, n * 128:(n + 1) * 128], wr[64:128, :],
                                       start=True, stop=True)
            ins.then_inc(sem("logit_ps"), 1)
            pe.wait_ge(sem("x2A"), 3)
            pe.wait_ge(sem("ld_w2"), 32)

            def up_proj(hf):
                for e in range(E):
                    for c in range(HC):
                        k = hf * E * HC + e * HC + c
                        if k >= 4:
                            pe.wait_ge(sem("hT"), k - 3)
                        nc.tensor.matmul(bk[:, 4 + k % 4, :], w1g[:, e, c * 128:(c + 1) * 128],
                                         x2A[:, hf * 512:(hf + 1) * 512], start=True, stop=True).then_inc(sem("hid_ps"), 1)

            def down_proj(hf):
                pe.wait_ge(sem("hT"), (hf + 1) * E * HC)
                for j in range(4):
                    n = hf * 4 + j
                    if n >= 2:
                        pe.wait_ge(sem("yw"), n - 1)
                    for e in range(E):
                        for c in range(HC):
                            ins = nc.tensor.matmul(bk[:, 2 + n % 2, e * D:(e + 1) * D], hT[:, e, c, j * 128:(j + 1) * 128],
                                                   w2[:, e, c, :], start=(c == 0), stop=(c == HC - 1))
                    ins.then_inc(sem("y_ps"), 1)

            up_proj(0)
            pe.wait_ge(sem("W8"), 1)
            for n in range(NT):
                ins = nc.tensor.transpose(bk[0:E, n // 4, (n % 4) * 128:(n % 4 + 1) * 128], W8[:, n, :], ident[:, :])
            ins.then_inc(sem("W8T_ps"), 1)
            down_proj(0)
            up_proj(1)
            pe.wait_ge(sem("W8T"), 2)
            for n in range(NT):
                ins = nc.tensor.matmul(bk[:, 0, n * D:(n + 1) * D], W8T[:, n * 128:(n + 1) * 128], b2[:, :],
                                       start=True, stop=True)
            ins.then_inc(sem("yb_ps"), 1)
            down_proj(1)

            pe.wait_ge(sem("ln"), 2)
            for n in range(NT):
                ins = nc.tensor.transpose(bk[0:D, 4 + n // 4, (n % 4) * 128:(n % 4 + 1) * 128], xn[:, n, :], ident[:, :])
                if n % 4 == 3:
                    ins.then_inc(sem("xcT_ps"), 1)
            pe.wait_ge(sem("xcT"), 2)
            for g in range(2):
                for q in range(B):
                    ins = nc.tensor.matmul(bk[32 * q:32 * q + 32, 2 + g, 0:S], c1a[:, 32 * g:32 * g + 32],
                                           xcT[:, q * S:(q + 1) * S], start=True, stop=True)
                ins.then_inc(sem("c1out"), 1)

            def taps(bank, kind, src, first, last):
                for k in range(9):
                    ins = nc.tensor.matmul(bk[:, bank, 0:S], cw[:, kind, k, :], src[:, k // 3:k // 3 + W, k % 3:k % 3 + W],
                                           start=(first and k == 0), stop=(last and k == 8), skip_group_check=True)
                return ins

            pe.wait_ge(sem("ld_cw"), 16)
            pe.wait_ge(sem("img"), 2)
            taps(0, 0, img[0], True, False)
            taps(0, 1, img[1], False, True).then_inc(sem("z_ps"), 1)
            taps(1, 3, img[1], True, False)
            pe.wait_ge(sem("z"), 1)
            taps(0, 2, zim[0], False, True).then_inc(sem("z_ps"), 1)
            pe.wait_ge(sem("z"), 2)
            taps(1, 4, zim[0], False, True).then_inc(sem("z_ps"), 1)
            pe.wait_ge(sem("z"), 3)
            taps(1, 5, zim[1], False, True).then_inc(sem("z_ps"), 1)
            for g in range(2):
                pe.wait_ge(sem("rz"), g + 1)
                for c in range(2):
                    ins = nc.tensor.transpose(bk[:, 2 + g, c * 128:(c + 1) * 128], rz[g][:, c * 128:(c + 1) * 128], ident[:, :])
                ins.then_inc(sem("A3_ps"), 1)

            pe.wait_ge(sem("ln"), 3)
            for n in range(NT):
                ins = nc.tensor.transpose(bk[0:D, 4 + n // 4, (n % 4) * 128:(n % 4 + 1) * 128], xn[:, n, :], ident[:, :])
                if n % 4 == 3:
                    ins.then_inc(sem("t3T_ps"), 1)
            pe.wait_ge(sem("ld_l"), 32)
            pe.wait_ge(sem("t3T"), 3)
            HU = LSTM_UN // 2

            def inputs_part(par, t):
                for g in range(3):
                    nc.tensor.matmul(bk[0:D, 3 * par + g, 0:HU * B], lu[:, g, :], t3T[:, bass.ds(t, HU), :] if not isinstance(t, int)
                                     else t3T[:, t:t + HU, :], start=True, stop=False, skip_group_check=True)

            inputs_part(0, 0)
            pe.wait_ge(sem("h_saved"), HU + 1)
            with nc.tensor.Fori(0, S, LSTM_UN) as i:
                for u in range(LSTM_UN):
                    for _ in range(FILL):
                        nc.tensor.matmul(bk[:, 7, 0:FILL_N], idle[:, 0:128], idle[:, 128:128 + FILL_N], start=True, stop=True)
                    pe.wait_ge(sem("h_new"), i + (u + 1))
                    for g in range(3):
                        nc.tensor.matmul(bk[0:D, 3 * (u // HU) + g, (u % HU) * B:(u % HU + 1) * B], lvh[:, g, :],
                                         hring[:, (u - 1) % LSTM_UN, :], start=False, stop=True,
                                         skip_group_check=True).then_inc(sem(f"gate{g}_ps"), 1)
                    if u == 1:
                        inputs_part(1, i + HU)
                    if u == HU + 1:
                        inputs_part(0, i + 2 * HU)
            pe.wait_ge(sem("h_saved"), S + HU + 1)
            for n in range(NT):
                b, c = n // 2, n % 2
                ins = nc.tensor.transpose(bk[:, 7, n * D:(n + 1) * D], hist[:, c * 128:(c + 1) * 128, b], ident[0:D, 0:D])
            ins.then_inc(sem("hs_ps"), 1)

        @block.scalar
        def _(act):
            def table(f):
                nc.scalar.activation(warm[:, 0:1], warm[:, 1:2], f)

            def root(n):
                act.wait_ge(sem("var"), n)
                nc.scalar.activation(sd[:, :], rs[:, :], ACT.Sqrt).then_inc(sem("std"), 1)

            act.wait_ge(sem("cleared"), 1)
            table(ACT.Sqrt)
            root(1)
            for n in range(2):
                act.wait_ge(sem("xnT_ps"), n + 1)
                nc.scalar.copy(xnT[:, n * 512:(n + 1) * 512], bk[0:D, n, :]).then_inc(sem("xnT"), 1)
            act.wait_ge(sem("qkv_ps"), 4)
            qkv = bk[:, 4:8, 0:384].rearrange("p k (n c) -> p k n c", n=2)
            nc.scalar.activation(qksq[:, :, :].rearrange("p (k n) c -> p k n c", n=2), qkv[:, :, :, 0:2 * D],
                                 ACT.Square).then_inc(sem("qksq"), 1)
            nc.scalar.copy(QV[:, :, D:2 * D].rearrange("p (k n) c -> p k n c", n=2), qkv[:, :, :, 2 * D:3 * D]).then_inc(sem("QV"), 1)
            act.wait_ge(sem("qk_sq"), 1)
            nc.scalar.activation(qkr[:, :, :], qkv2[:, :, :], ACT.Sqrt).then_inc(sem("qk_n"), 1)
            table(ACT.Gelu_apprx_tanh)
            for n in range(2):
                act.wait_ge(sem("glog"), n + 1)
                nc.scalar.activation(gS[:, n * 512:(n + 1) * 512], bk[0:3, 2 + n, :], ACT.Tanh, scale=0.5).then_inc(sem("gS"), 1)
            act.wait_ge(sem("kkT_ps"), 1)
            for n in range(2):
                nc.scalar.copy(kk[:, 2 * n:2 * n + 2, 0:S], bk[:, n, :].rearrange("p (b s) -> p b s", b=2)).then_inc(sem("kkT"), 1)
            act.wait_ge(sem("qvT_ps"), 1)
            for n in range(2):
                nc.scalar.copy(vT[:, 2 * n:2 * n + 2, 0:S], bk[:, 4 + n, :].rearrange("p (b s) -> p b s", b=2)).then_inc(sem("kkT"), 1)
            for n in range(2):
                nc.scalar.copy(qq[0:D, n * 512:(n + 1) * 512], bk[0:D, 4 + n, :]).then_inc(sem("qq"), 1)

            def tokens(t):
                return t.rearrange("p (b c) -> p b c", b=B)[:, :, 0:C]

            with nc.scalar.Fori(0, T, MEM_UN) as i:
                for u in range(MEM_UN):
                    t1 = i + (u + 1)
                    lr = lrcur[u % 2][:, 0:1]
                    act.wait_ge(sem("a0tok"), t1)
                    nc.scalar.activation(g0tok[:, :], bk[:, 1, 0:DE], ACT.Gelu_apprx_tanh).then_inc(sem("g0tok"), 1)
                    nc.scalar.activation(a0q[:, :], bk[:, 1, 0:DE], ACT.Square).then_inc(sem("a0q"), 1)
                    act.wait_ge(sem("ktok_ps"), t1)
                    nc.scalar.activation(ktok[:, :], bk[:, 2, 448:448 + D], ACT.Copy, scale=lr).then_inc(sem("ktok"), 1)
                    act.wait_ge(sem("g0T_ps"), t1)
                    nc.scalar.copy(g0T[:, :, :], tokens(bk[:, 0, 0:128])).then_inc(sem("g0T"), 1)
                    act.wait_ge(sem("w11T_ps"), t1)
                    nc.scalar.copy(w11T[:, :, :].rearrange("p b e -> p (b e)"), bk[:, 3, 256:512]).then_inc(sem("w11T"), 1)
                    act.wait_ge(sem("a0u"), t1)
                    nc.scalar.activation(a0t[:, :], a0u[:, :], ACT.Tanh, scale=RT2PI * KAPPA).then_inc(sem("a0t"), 1)
                    act.wait_ge(sem("a0t"), t1)
                    nc.scalar.activation(a0s[:, :], a0t[:, :], ACT.Square).then_inc(sem("a0tq"), 1)
                    act.wait_ge(sem("w21T_ps"), t1)
                    nc.scalar.mul(w21T[64:128, :, :].rearrange("p b e -> p (b e)"), bk[0:D, 4, :], 0.5).then_inc(sem("w21T"), 1)
                    act.wait_ge(sem("a1tok"), t1)
                    nc.scalar.activation(g1tok[:, :], bk[:, 3, 0:DE], ACT.Gelu_apprx_tanh).then_inc(sem("g1tok"), 1)
                    nc.scalar.activation(a1q[:, :], bk[:, 3, 0:DE], ACT.Square).then_inc(sem("a1q"), 1)
                    act.wait_ge(sem("g1T_ps"), t1)
                    nc.scalar.copy(g1T[:, :, :], tokens(bk[:, 1, 128:256])).then_inc(sem("g1T"), 1)
                    act.wait_ge(sem("h1tok_ps"), t1)
                    nc.scalar.activation(h1tok[:, :], bk[:, 0, 128:128 + D], ACT.Copy, scale=lr).then_inc(sem("h1tok"), 1)
                    act.wait_ge(sem("a1u"), t1)
                    nc.scalar.activation(a1t[:, :], a1u[:, :], ACT.Tanh, scale=RT2PI * KAPPA).then_inc(sem("a1t"), 1)
                    act.wait_ge(sem("a1t"), t1)
                    nc.scalar.activation(a1s[:, :], a1t[:, :], ACT.Square).then_inc(sem("a1tq"), 1)
                    act.wait_ge(sem("w20T_ps"), t1)
                    nc.scalar.mul(w20T[64:128, :, :].rearrange("p b e -> p (b e)"), bk[0:D, 6, :], 0.5).then_inc(sem("w20T"), 1)
                    act.wait_ge(sem("dtok_ps"), t1)
                    nc.scalar.activation(dtok[:, :], bk[:, 0, 192:192 + D], ACT.Copy, scale=lr).then_inc(sem("dtok"), 1)
                    act.wait_ge(sem("da1T_ps"), t1)
                    nc.scalar.copy(da1T[:, :, :], tokens(bk[:, 1, 256:384])).then_inc(sem("da1T"), 1)
                    act.wait_ge(sem("dh1tok_ps"), t1)
                    nc.scalar.activation(dh1tok[:, :], bk[:, 0, 256:256 + D], ACT.Copy, scale=lr).then_inc(sem("dh1tok"), 1)

            for n in range(2):
                act.wait_ge(sem("f_a0"), n + 1)
                nc.scalar.activation(g0F[:, n * 512:(n + 1) * 512], bk[:, 2 + n, :], ACT.Gelu_apprx_tanh).then_inc(sem("f_g0"), 1)
            for n in range(2):
                act.wait_ge(sem("f_a1"), n + 1)
                nc.scalar.activation(g1F[:, n * 512:(n + 1) * 512], bk[:, 6 + n, :], ACT.Gelu_apprx_tanh).then_inc(sem("f_g1"), 1)
            table(ACT.Sqrt)
            for k, dst in enumerate((c1a, c1b, c1a)):
                act.wait_ge(sem("c1_ps"), k + 1)
                nc.scalar.copy(dst[:, :], bk[0:D + 1, 2 + k % 2, 0:D + 1]).then_inc(sem("c1"), 1)
                if k == 0:
                    act.wait_ge(sem("w1row_ps"), 1)
                    act.wait_ge(sem("w1g"), 1)
                    nc.scalar.copy(w1g[D:D + 1, :, :].rearrange("p (k n) h -> p k (n h)", k=4), bk[64:65, 4:8, :]).then_inc(sem("w1row"), 1)
            root(2)
            root(3)
            table(ACT.Gelu)

            for n in range(2):
                act.wait_ge(sem("XT_ps"), n + 1)
                nc.scalar.copy(t1T[64:128, n * 512:(n + 1) * 512], bk[64:128, 2 + n, :]).then_inc(sem("t1T"), 1)
                nc.scalar.copy(x2A[0:D, n * 512:(n + 1) * 512], bk[0:D, 2 + n, :]).then_inc(sem("x2A"), 1)

            def gelus(hf):
                if hf == 1:
                    act.wait_ge(sem("y_ps"), 4)
                for k in range(hf * E * HC, (hf + 1) * E * HC):
                    e, c = k % (E * HC) // HC, k % HC
                    act.wait_ge(sem("hid_ps"), k + 1)
                    nc.scalar.activation(hT[:, e, c, :], bk[:, 4 + k % 4, :], ACT.Gelu).then_inc(sem("hT"), 1)

            act.wait_ge(sem("md"), 1)
            nc.scalar.activation(p1[:, :], md[:, :], ACT.Tanh, scale=0.5).then_inc(sem("p12"), 1)
            gelus(0)
            act.wait_ge(sem("W8T_ps"), 1)
            for n in range(2):
                nc.scalar.copy(W8T[:, n * 512:(n + 1) * 512], bk[0:E, n, :]).then_inc(sem("W8T"), 1)
            gelus(1)

            table(ACT.Sqrt)
            root(4)
            for n in range(2):
                act.wait_ge(sem("xcT_ps"), n + 1)
                nc.scalar.copy(xcT[0:D, n * 512:(n + 1) * 512], bk[0:D, 4 + n, :]).then_inc(sem("xcT"), 1)
            for g in range(2):
                act.wait_ge(sem("c1out"), g + 1)
                nc.scalar.activation(inner(img[g]), bk[:, 2 + g, 0:S].rearrange("p (y x) -> p y x", x=W), ACT.Relu).then_inc(sem("img"), 1)
            act.wait_ge(sem("ld_3"), 48)
            act.wait_ge(sem("z"), 2)
            nc.scalar.activation(rz[0][:, :], bk[:, 0, 0:S], ACT.Relu, bias=cb2[:, 0:1]).then_inc(sem("rz"), 1)
            act.wait_ge(sem("z_ps"), 4)
            nc.scalar.activation(rz[1][:, :], bk[:, 1, 0:S], ACT.Relu, bias=cb2[:, 0:1]).then_inc(sem("rz"), 1)

            root(5)
            table(ACT.Tanh)
            act.wait_ge(sem("rec_init"), 1)
            HU = LSTM_UN // 2
            with nc.scalar.Fori(0, S, LSTM_UN) as i:
                for u in range(LSTM_UN):
                    t1 = i + (u + 1)
                    cols = slice((u % HU) * B, (u % HU + 1) * B)
                    bank = 3 * (u // HU)
                    act.wait_ge(sem("gate0_ps"), t1)
                    nc.scalar.activation(gp[:, :, 0:2], wide(bk[0:D, bank, cols], 2), ACT.Tanh)
                    act.wait_ge(sem("gate1_ps"), t1)
                    nc.scalar.activation(bk[0:D, 6, 1:3 * B:3], bk[0:D, bank + 1, cols], ACT.Tanh, scale=0.5).then_inc(sem("in_gate"), 1)
                    act.wait_ge(sem("gate2_ps"), t1)
                    nc.scalar.activation(og[:, :], bk[0:D, bank + 2, cols], ACT.Tanh, scale=0.5)
                    act.wait_ge(sem("c_new"), t1)
                    nc.scalar.activation(bk[0:D, 6, 16:16 + B], cs[u % 2][:, :, 2], ACT.Tanh, scale=0.5).then_inc(sem("tanh_c"), 1)

        @block.vector
        def _(dve):
            links, norms = [0], [0]

            def link(ins):
                links[0] += 1
                ins.then_inc(sem("dve"), 1)
                dve.wait_ge(sem("dve"), links[0])

            def newton(y, v, tmp):
                link(nc.vector.tensor_tensor(tmp, y, y, ALU.mult))
                link(nc.vector.scalar_tensor_tensor(tmp, tmp, -0.5, v, ALU.mult, ALU.mult))
                link(nc.vector.scalar_tensor_tensor(y, tmp, 1.5, y, ALU.add, ALU.mult))

            def rstd():
                norms[0] += 1
                dve.wait_ge(sem("std"), norms[0])
                link(nc.vector.reciprocal(sd[:, :], sd[:, :]))
                newton(sd[:, :], rs[:, :], nt[:, 0:NT])

            def norm(src, dst, eps, signal):
                for n in range(NT):
                    ins = nc.vector.bn_stats(bst[:, n, :], src[:, n, :])
                link(ins)
                for n in range(NT):
                    ins = nc.vector.bn_aggr(mv[:, n, :], bst[:, n, :])
                link(ins)
                nc.vector.tensor_scalar(rs[:, :], mv[:, :, 1], eps, None, ALU.add).then_inc(sem("var"), 1)
                nc.vector.tensor_tensor(xc[:, :, :], src, wide(mv[:, :, 0], D), ALU.subtract)
                rstd()
                ins = nc.vector.tensor_tensor(dst, xc[:, :, :], wide(sd[:, :], D), ALU.mult)
                if signal:
                    ins.then_inc(sem(signal), 1)
                return ins

            dve.wait_ge(sem("ld_x"), 16)
            norm(xs[:, :, :], xn[:, :, :], 1e-6, "ln")
            dve.wait_ge(sem("qksq"), 1)
            link(nc.vector.tensor_reduce(qkr[:, :, :], qksq[:, :, :].rearrange("p n (a c) -> p n a c", a=2), AX, ALU.add))
            nc.vector.tensor_scalar(qkv2[:, :, :], qkr[:, :, :], 1e-24, None, ALU.max).then_inc(sem("qk_sq"), 1)
            dve.wait_ge(sem("qk_n"), 1)
            link(nc.vector.reciprocal(qkr[:, :, :], qkr[:, :, :]))
            newton(qkr[:, :, :], qkv2[:, :, :], nt[:, :].rearrange("p (n a) -> p n a", a=2))
            qkv = bk[:, 4:8, 0:384].rearrange("p k (n c) -> p k n c", n=2)

            def unit(dst, a):
                return nc.vector.tensor_tensor(dst.rearrange("p (k n) c -> p k n c", n=2), qkv[:, :, :, a * D:(a + 1) * D],
                                               wide(qkr[:, :, a].rearrange("p (k n) -> p k n", n=2), D), ALU.mult)

            unit(KK[:, :, 0:D], 1)
            unit(KK[:, :, D:2 * D], 1).then_inc(sem("KK"), 1)
            unit(QV[:, :, 0:D], 0).then_inc(sem("QV"), 1)
            dve.wait_ge(sem("ld_g"), 32)
            dve.wait_ge(sem("gS"), 2)
            link(nc.vector.tensor_reduce(gsum[:, :], gS[:, :].rearrange("p (s c) -> p s c", c=C), AX, ALU.add))
            nc.vector.tensor_scalar(glin[:, :], gsum[:, :], gaff[:, 0:1], gaff[:, 1:2], ALU.mult, ALU.add).then_inc(sem("glin"), 1)
            dve.wait_ge(sem("cleared"), 1)
            dve.wait_ge(sem("gate_ps"), 1)
            nc.vector.tensor_copy(gates[:, :, :, 0:T], bk[:, 2, 0:3 * B * T].rearrange("p (g b t) -> p g b t", g=3, b=B)).then_inc(sem("gates"), 1)
            dve.wait_ge(sem("gates"), 1)
            for b in range(B):
                r = slice(32 * b, 32 * b + 32)
                nc.vector.tensor_copy(lrtok[r, 0:T], gates[r, 2, b, 0:T]).then_inc(sem("gates"), 1)
            dve.wait_ge(sem("kkT"), 4)
            dve.wait_ge(sem("qq"), 2)
            nc.vector.memset(bk[:, 0:4, :], 0.0).then_inc(sem("ps_clear"), 1)
            dve.wait_ge(sem("ld_m"), 16)
            nc.vector.tensor_copy(P[:, :, :], mid(memw[:, :], B)).then_inc(sem("p1_new"), 1)
            dve.wait_ge(sem("p1_new"), 1)
            nc.vector.memset(og[:, :], 0.0).then_inc(sem("p2_new"), 1)
            nc.vector.memset(a0x[:, :], 0.0).then_inc(sem("m_new"), 1)

            with nc.vector.Fori(0, T, MEM_UN) as i:
                for u in range(MEM_UN):
                    t1 = i + (u + 1)
                    kc, vc = kcur[u % 2], vcur[u % 2]
                    dve.wait_ge(sem("a0q"), t1)
                    nc.vector.scalar_tensor_tensor(a0u[:, :], a0q[:, :], 1.0 / KAPPA, bk[:, 1, 0:DE], ALU.add, ALU.mult).then_inc(sem("a0u"), 1)
                    nc.vector.scalar_tensor_tensor(a0y[:, :], a0q[:, :], 1.0 / (3 * KAPPA), bk[:, 1, 0:DE], ALU.add, ALU.mult).then_inc(sem("a0y"), 1)
                    dve.wait_ge(sem("h1_ps"), t1)
                    nc.vector.tensor_tensor(h1T[64:128, :, 0:C], bk[64:128, 2, 0:64].rearrange("p (b c) -> p b c", b=B),
                                            kc[64:128, :, 0:C], ALU.add).then_inc(sem("h1T"), 1)
                    dve.wait_ge(sem("h1T"), t1)
                    nc.vector.tensor_tensor(hv[64:128, :, :], h1T[64:128, :, 0:C], vc[64:128, :, :], ALU.subtract).then_inc(sem("hv"), 1)
                    dve.wait_ge(sem("a0tq"), t1)
                    nc.vector.scalar_tensor_tensor(a0y[:, :], a0s[:, :], -1.0, a0y[:, :], ALU.add, ALU.mult).then_inc(sem("a0z"), 1)
                    dve.wait_ge(sem("a0z"), t1)
                    nc.vector.scalar_tensor_tensor(a0x[:, :], a0y[:, :], -3 * KAPPA * RT2PI, a0t[:, :], ALU.mult, ALU.add).then_inc(sem("a0x"), 1)
                    dve.wait_ge(sem("a1q"), t1)
                    nc.vector.scalar_tensor_tensor(a1u[:, :], a1q[:, :], 1.0 / KAPPA, bk[:, 3, 0:DE], ALU.add, ALU.mult).then_inc(sem("a1u"), 1)
                    nc.vector.scalar_tensor_tensor(a1y[:, :], a1q[:, :], 1.0 / (3 * KAPPA), bk[:, 3, 0:DE], ALU.add, ALU.mult).then_inc(sem("a1y"), 1)
                    dve.wait_ge(sem("hv"), t1)
                    dve.wait_ge(sem("pred_ps"), t1)
                    nc.vector.tensor_tensor(dT[64:128, :, 0:C], bk[64:128, 2, 64:128].rearrange("p (b c) -> p b c", b=B),
                                            hv[64:128, :, :], ALU.add).then_inc(sem("dT"), 1)
                    dve.wait_ge(sem("a1y"), t1)
                    dve.wait_ge(sem("a1tq"), t1)
                    nc.vector.scalar_tensor_tensor(a1y[:, :], a1s[:, :], -1.0, a1y[:, :], ALU.add, ALU.mult).then_inc(sem("a1z"), 1)
                    dve.wait_ge(sem("a1z"), t1)
                    nc.vector.scalar_tensor_tensor(a1x[:, :], a1y[:, :], -3 * KAPPA * RT2PI, a1t[:, :], ALU.mult, ALU.add).then_inc(sem("a1x"), 1)
                    dve.wait_ge(sem("a1x"), t1)
                    dve.wait_ge(sem("dg1_ps"), t1)
                    nc.vector.scalar_tensor_tensor(da1tok[:, :], a1x[:, :], 1.0, bk[:, 2, 128:128 + DE], ALU.add, ALU.mult).then_inc(sem("da1tok"), 1)
                    dve.wait_ge(sem("dh1_ps"), t1)
                    nc.vector.tensor_tensor(dh1T[64:128, :, 0:C], bk[64:128, 2, 256:320].rearrange("p (b c) -> p b c", b=B),
                                            dT[64:128, :, 0:C], ALU.add).then_inc(sem("dh1T"), 1)
                    dve.wait_ge(sem("dg0_ps"), t1)
                    nc.vector.scalar_tensor_tensor(da0tok[:, :], a0x[:, :], 1.0, bk[:, 2, 320:320 + DE], ALU.add, ALU.mult).then_inc(sem("da0tok"), 1)
                    dve.wait_ge(sem("Q"), t1)
                    dve.wait_ge(sem("grads"), t1)
                    nc.vector.tensor_tensor(P[:, :, 0:DE], Q[:, :, 0:DE], bk[:, 4:8, 0:DE], ALU.add).then_inc(sem("p1_new"), 1)
                    nc.vector.tensor_tensor(P[:, :, DE:2 * DE], Q[:, :, DE:2 * DE], bk[:, 4:8, DE:2 * DE], ALU.add).then_inc(sem("p2_new"), 1)
                    nc.vector.tensor_tensor(M[:, :, :], Me[:, :, :], bk[:, 4:8, 0:2 * DE], ALU.add).then_inc(sem("m_new"), 1)

            dve.wait_ge(sem("zeros"), 1)
            nc.vector.memset(x2A[D:D + 1, :], 1.0).then_inc(sem("x2A"), 1)
            dve.wait_ge(sem("m_new"), T + 1)
            link(nc.vector.tensor_tensor(FW2[:, :, :], P[:, 0:2, :], P[:, 2:4, :], ALU.add))
            link(nc.vector.tensor_tensor(FW[:, :], FW2[:, 0, :], FW2[:, 1, :], ALU.add))
            nc.vector.tensor_scalar(FW[:, :], FW[:, :], 1.0 / B, None, ALU.mult).then_inc(sem("FW"), 1)
            dve.wait_ge(sem("ld_3"), 48)
            nc.vector.tensor_scalar(sc0[:, :, 1:D], mid(w3[:, 0:D - 1], NT), 1.0, None, ALU.add)
            for n in range(2):
                dve.wait_ge(sem("f_h1_ps"), n + 1)
                nc.vector.tensor_tensor(h1F[64:128, n * 512:(n + 1) * 512], bk[64:128, 4 + n, :], qq[0:D, n * 512:(n + 1) * 512],
                                        ALU.add).then_inc(sem("f_h1"), 1)
            for n in range(2):
                dve.wait_ge(sem("f_y"), n + 1)
                ins = nc.vector.tensor_tensor(xs[:, 4 * n:4 * n + 4, :], xs[:, 4 * n:4 * n + 4, :],
                                              bk[:, n, 0:4 * D].rearrange("p (n d) -> p n d", n=4), ALU.add)
                link(ins)

            link(norm(xs[:, :, :], XT[:, :, D:2 * D], 1e-5, None))
            link(nc.vector.tensor_tensor(st[:, :], sd[:, :], sd[:, :], ALU.mult))
            link(nc.vector.tensor_tensor(rs[:, :], mv[:, :, 1], st[:, :], ALU.mult))
            nc.vector.tensor_scalar(rs[:, :], rs[:, :], 1e-5, None, ALU.add).then_inc(sem("var"), 1)
            rstd()
            nc.vector.tensor_tensor(XT[:, :, 0:D], XT[:, :, D:2 * D], wide(sd[:, :], D), ALU.mult).then_inc(sem("XT"), 1)
            dve.wait_ge(sem("logit_ps"), 1)
            link(nc.vector.tensor_tensor(L[:, :, :], bk[:, 0, 0:NT * E].rearrange("p (n e) -> p n e", n=NT), mid(br[:, :], NT), ALU.add))

            def first_max(src, m, pick):
                link(nc.vector.tensor_reduce(m[:, :], src[:, :, :], AX, ALU.max))
                link(nc.vector.tensor_tensor(eq[:, :, :], src[:, :, :], wide(m[:, :], E), ALU.is_equal))
                flat = "p n e -> p (n e)"
                link(nc.vector.tensor_tensor_scan(cum[:, :, :].rearrange(flat), notfirst[:, :], eq[:, :, :].rearrange(flat),
                                                  0.0, ALU.mult, ALU.add))
                link(nc.vector.scalar_tensor_tensor(pick[:, :, :], cum[:, :, :], 1.0, eq[:, :, :], ALU.is_equal, ALU.mult))

            first_max(L, m1, pick1)
            link(nc.vector.scalar_tensor_tensor(L2[:, :, :], pick1[:, :, :], -3.0e38, L[:, :, :], ALU.mult, ALU.add))
            first_max(L2, m2, pick2)
            nc.vector.tensor_tensor(md[:, :], m1[:, :], m2[:, :], ALU.subtract).then_inc(sem("md"), 1)
            dve.wait_ge(sem("p12"), 1)
            nc.vector.tensor_scalar(p2[:, :], p1[:, :], -0.5, 0.5, ALU.mult, ALU.add)
            link(nc.vector.tensor_scalar(p1[:, :], p1[:, :], 0.5, 0.5, ALU.mult, ALU.add))
            link(nc.vector.tensor_tensor(pick1[:, :, :], pick1[:, :, :], wide(p1[:, :], E), ALU.mult))
            link(nc.vector.tensor_tensor(pick2[:, :, :], pick2[:, :, :], wide(p2[:, :], E), ALU.mult))
            nc.vector.tensor_tensor(W8[:, :, :], pick1[:, :, :], pick2[:, :, :], ALU.add).then_inc(sem("W8"), 1)

            def combine(hf):
                for j in range(4):
                    n = hf * 4 + j
                    dve.wait_ge(sem("y_ps"), n + 1)
                    nc.vector.tensor_tensor(yw[n % 2][:, :, :], bk[:, 2 + n % 2, :].rearrange("p (e d) -> p e d", e=E),
                                            wide(W8[:, n, :], D), ALU.mult).then_inc(sem("yw"), 1)
                    dve.wait_ge(sem("yw"), n + 1)
                    nc.vector.tensor_reduce(ysum[:, n, :], yw[n % 2][:, :, :].rearrange("p e d -> p d e"), AX, ALU.add).then_inc(sem("ysum"), 1)

            dve.wait_ge(sem("W8"), 1)
            combine(0)
            dve.wait_ge(sem("yb_ps"), 1)
            link(nc.vector.tensor_tensor(xs[:, :, :], xs[:, :, :], bk[:, 0, :].rearrange("p (n d) -> p n d", n=NT), ALU.add))
            combine(1)
            dve.wait_ge(sem("ysum"), NT)
            link(nc.vector.tensor_tensor(xs[:, :, :], xs[:, :, :], ysum[:, :, :], ALU.add))

            norm(xs[:, :, :], xn[:, :, :], 1e-6, "ln")
            for k, (need, bank) in enumerate(((1, 0), (2, 0), (3, 1))):
                dve.wait_ge(sem("z_ps"), need)
                nc.vector.tensor_scalar(inner(zim[bank]), bk[:, bank, 0:S].rearrange("p (y x) -> p y x", x=W), cb2[:, 0:1], None,
                                        ALU.add).then_inc(sem("z"), 1)
            for g in range(2):
                dve.wait_ge(sem("A3_ps"), g + 1)
                for c in range(2):
                    ins = nc.vector.tensor_copy(A3[:, c::2, 32 * g:32 * g + 32],
                                                bk[:, 2 + g, c * 128:(c + 1) * 128].rearrange("p (q o) -> p q o", q=B))
                link(ins)
            link(nc.vector.tensor_tensor(prod[:, :, :], A3[:, :, :], mid(w3[:, :], NT), ALU.mult))
            link(nc.vector.tensor_reduce(st[:, :], prod[:, :, :], AX, ALU.add))
            link(nc.vector.tensor_scalar(sc1[:, :, 1:D], prod[:, :, 0:D - 1], -1.0, None, ALU.mult))
            link(nc.vector.tensor_scalar(sc1[:, :, 0:1], wide(st[:, :], 1), b3[:, 0:1], None, ALU.add))
            fl = "p n d -> p (n d)"
            link(nc.vector.tensor_tensor_scan(prod[:, :, :].rearrange(fl), sc0[:, :, :].rearrange(fl), sc1[:, :, :].rearrange(fl),
                                              0.0, ALU.mult, ALU.add))
            link(nc.vector.tensor_tensor(xs[:, :, :], xs[:, :, :], xn[:, :, :], ALU.add))
            link(nc.vector.tensor_tensor(xs[:, :, :], xs[:, :, :], prod[:, :, :], ALU.add))

            norm(xs[:, :, :], xn[:, :, :], 1e-5, "ln")
            for n in range(2):
                dve.wait_ge(sem("t3T_ps"), n + 1)
                for c in range(2):
                    ins = nc.vector.tensor_copy(
                        t3T[0:D, c * 128:(c + 1) * 128, 2 * n:2 * n + 2].rearrange("p s b -> p b s"),
                        bk[0:D, 4 + n, :].rearrange("p (b c s) -> p b c s", b=2, c=2)[:, :, c, :])
                ins.then_inc(sem("t3T"), 1)
            nc.vector.memset(t3T[D:D + 1, :, :], 1.0).then_inc(sem("t3T"), 1)
            dve.wait_ge(sem("ld_l"), 32)
            nc.vector.memset(lvh[D:D + 1, :, :], 0.0)
            nc.vector.tensor_scalar(lvh[0:D, :, :], lv[:, :, :], 0.5, None, ALU.mult)
            link(nc.vector.memset(bk[0:D, 6, 0:32], 0.0))
            nc.vector.memset(bk[0:D, 6, 2:3 * B:3], 1.0).then_inc(sem("rec_init"), 1)
            nc.vector.memset(og[:, :], 0.0).then_inc(sem("h_new"), 1)
            HU = LSTM_UN // 2
            flat3 = "p b k -> p (b k)"
            with nc.vector.Fori(0, S, LSTM_UN) as i:
                for u in range(LSTM_UN):
                    t1 = i + (u + 1)
                    c_t = cs[u % 2]
                    if u % HU == 0:
                        dve.wait_ge(sem("h_saved"), i + (u + 1))
                    dve.wait_ge(sem("in_gate"), t1)
                    nc.vector.tensor_tensor_scan(c_t[:, :, :].rearrange(flat3), bk[0:D, 6, 0:3 * B], gp[:, :, :].rearrange(flat3),
                                                 0.0, ALU.mult, ALU.add).then_inc(sem("c_new"), 1)
                    dve.wait_ge(sem("tanh_c"), t1)
                    nc.vector.scalar_tensor_tensor(hring[0:D, u, :], og[:, :], 1.0, bk[0:D, 6, 16:16 + B],
                                                   ALU.add, ALU.mult).then_inc(sem("h_new"), 1)
                    dve.wait_ge(sem("h_new"), i + (u + 2))
                    nc.vector.scalar_tensor_tensor(gp[:, :, 2], hring[0:D, u, :], 0.5, c_t[:, :, 2], ALU.mult, ALU.mult).then_inc(sem("hc"), 1)
                    dve.wait_ge(sem("hc"), t1)

            dve.wait_ge(sem("hs_ps"), 1)
            nc.vector.scalar_tensor_tensor(xs[:, :, :], bk[:, 7, :].rearrange("p (n d) -> p n d", n=NT), 0.5, xs[:, :, :],
                                           ALU.mult, ALU.add).then_inc(sem("x_done"), 1)


def layouts(a):
    f = np.float32
    x = np.asarray(a["x"], f)
    o = {"x": np.ascontiguousarray(x.reshape(NT, 128, D).transpose(1, 0, 2))}
    o["ident"] = np.eye(128, dtype=f)
    o["wqkv"] = np.concatenate([a["L0_conv_Wq"], a["L0_conv_Wk"], a["L0_conv_Wv"]], axis=1)
    o["wgate"] = np.stack([a["L0_conv_w_eta"], a["L0_conv_w_forget"], a["L0_conv_w_lr"]], axis=1)
    lr = -0.1 * 2.0 / (C * D)
    o["gaff"] = np.array([[0.5 / C, 0.5], [-0.5 / C, 0.5], [lr * 0.5 / C, lr * 0.5]], f)
    o["gsel"] = np.repeat(np.eye(3, dtype=f)[:, :, None], 128, axis=2)
    o["memw"] = np.concatenate([np.concatenate([a["L0_conv_w1_0"], a["L0_conv_w1_1"]], axis=0),
                                a["L0_conv_w2_0"], a["L0_conv_w2_1"]], axis=1)
    o["wr"] = np.asarray(a["L0_ffn_Wr"])
    o["br"] = np.repeat(np.asarray(a["L0_ffn_br"])[None, :], 128, axis=0)
    o["lng"] = np.asarray(a["L0_ffn_ln_g"]).T
    o["lnb"] = np.concatenate([np.asarray(a["L0_ffn_ln_b"]).T, np.ones((1, E), f)], axis=0)
    o["w1"] = np.concatenate([np.asarray(a["L0_ffn_W1"]).transpose(1, 0, 2), np.asarray(a["L0_ffn_b1"])[None]], axis=0)
    o["w2"] = np.asarray(a["L0_ffn_W2"]).reshape(E, HC, 128, D).transpose(2, 0, 1, 3)
    o["b2"] = np.asarray(a["L0_ffn_b2"])
    nf = np.ones((128, NT, E), f)
    nf[:, :, 0] = 0.0
    o["notfirst"] = nf.reshape(128, NT * E)
    w1, b1 = np.asarray(a["L1_conv_w1"])[0, 0], np.asarray(a["L1_conv_b1"])[0, 0, 0]
    ps = np.zeros((4, D + 1, D + 1), f)
    for g in range(4):
        ps[g] = np.eye(D + 1, dtype=f)
        ps[g][:, 16 * g:16 * g + 16] = np.concatenate([w1, b1[None, :]], axis=0)
    o["c1p"] = ps.transpose(2, 0, 1)
    o["c1last"] = ps[3]
    w2 = np.asarray(a["L1_conv_w2"]).reshape(9, D, 16).transpose(1, 0, 2)
    cw = np.zeros((6, B, 32, 9, B, 2, 16), f)
    for q in range(B):
        lo, hi = w2[0:32], w2[32:64]
        cw[0, q, :, :, q, 0] = lo
        cw[0, q, 16:, :, q, 1] = lo[16:]
        cw[1, q, :, :, q, 0] = hi
        cw[1, q, :, :, q, 1] = hi
        cw[2, q, :16, :, q, 1] = lo[:16]
        cw[3, q, :, :, q, 0] = hi
        cw[3, q, 16:, :, q, 1] = hi[16:]
        cw[4, q, :, :, q, 0] = lo
        cw[4, q, :, :, q, 1] = lo
        cw[5, q, :16, :, q, 1] = hi[:16]
    o["cw"] = cw.reshape(6, 128, 9, 128).transpose(1, 0, 2, 3)
    o["cb2"] = np.tile(np.asarray(a["L1_conv_b2"]).reshape(16), 8)[:, None]
    o["w3"] = np.repeat(np.asarray(a["L1_conv_w3"]).reshape(1, D), 128, axis=0)
    o["b3"] = np.repeat(np.asarray(a["L1_conv_b3"]).reshape(1, 1), 128, axis=0)
    o["lu"] = np.stack([np.concatenate([a["L1_ffn_U_" + g], np.asarray(a["L1_ffn_b_" + g])[None]], axis=0) for g in "cio"], axis=1)
    o["lv"] = np.stack([np.asarray(a["L1_ffn_V_" + g]) for g in "cio"], axis=1)
    return {k: np.ascontiguousarray(v) for k, v in o.items()}


def kernel(**inputs):
    import concourse.bacc as _bacc
    from concourse.bass_utils import run_bass_kernel_spmd as _run

    nc = _bacc.Bacc("TRN2", target_bir_lowering=False, num_devices=1)
    arrays, aps = {}, {}
    for name, v in layouts(inputs).items():
        arrays[f"in_{name}"] = v
        aps[name] = nc.dram_tensor(f"in_{name}", v.shape, mybir.dt.from_np(v.dtype), kind="ExternalInput").ap()
    out = nc.dram_tensor("out", (128, NT, D), F32, kind="ExternalOutput").ap()
    build(nc, aps, out)
    r = _run(nc, [arrays], core_ids=[0])
    got = r.results[0]["out"]
    return np.ascontiguousarray(got.transpose(1, 0, 2)).reshape(B, T, C, D)
```

```python
from contextlib import ExitStack

import concourse.bass as bass
from concourse import mybir
import numpy as np

F32 = mybir.dt.float32
ALU = mybir.AluOpType
ACT = mybir.ActivationFunctionType
AX = mybir.AxisListType.X

B, T, C, D = 4, 16, 16, 64
DE = 128
NTOK = B * T * C
NT = NTOK // 128
E, H, HC = 8, 256, 2
W = 16
S = W * W
PADW = W + 2
KAPPA = 0.044715
RT2PI = float(np.sqrt(2.0 / np.pi))
LSTM_UN = 32
FILL, FILL_N = 4, 512
LEAD = 6
AFTER = (8, 14, 10, 4, 0, 20, 4, 28)
BUSY = (10, 4, 4, 2, 2, 0, 5, 5, 4, 0, 4, 2)
MEM_UN = 4
TP = T + MEM_UN


def wide(ap, n):
    return bass.AP(ap.tensor, ap.offset, [*ap.ap, [0, n]])


def mid(ap, n):
    return bass.AP(ap.tensor, ap.offset, [ap.ap[0], [0, n], *ap.ap[1:]])


def build(nc, i_, out):
    with ExitStack() as ctx:
        def sb(name, shape):
            return ctx.enter_context(nc.sbuf_tensor(name, shape, F32))

        names = {}

        def sem(name):
            if name not in names:
                names[name] = ctx.enter_context(nc.semaphore(name))
            return names[name]

        bk = ctx.enter_context(nc.psum_tensor("bk", [128, 8, 512], F32))

        ident = sb("ident", [128, 128])
        wqkv = sb("wqkv", [128, 3 * D])
        wgate = sb("wgate", [128, 3])
        gaff = sb("gaff", [3, 2])
        gsel = sb("gsel", [3, 3, 128])
        memw = sb("memw", [128, 2 * DE])
        wr = sb("wr", [128, E])
        br = sb("br", [128, E])
        lng = sb("lng", [D, E])
        lnb = sb("lnb", [D + 1, E])
        w1 = sb("w1", [D + 1, E, H])
        w1g = sb("w1g", [128, E, H])
        w2 = sb("w2", [128, E, HC, D])
        b2 = sb("b2", [E, D])
        c1p = sb("c1p", [D + 1, 4, D + 1])
        c1last = sb("c1last", [D + 1, D + 1])
        cw = sb("cw", [128, 6, 9, 128])
        cb2 = sb("cb2", [128, 1])
        w3 = sb("w3", [128, D])
        b3 = sb("b3", [128, 1])
        lu = sb("lu", [D + 1, 3, D])
        lv = sb("lv", [D, 3, D])
        notfirst = sb("notfirst", [128, NT * E])

        xs = sb("xs", [128, NT, D])
        xc = sb("xc", [128, NT, D])
        bst = sb("bst", [128, NT, 6])
        mv = sb("mv", [128, NT, 2])
        xn = sb("xn", [128, NT, D])
        st = sb("st", [128, NT])
        rs = sb("rs", [128, NT])
        sd = sb("sd", [128, NT])
        nt = sb("nt", [128, 2 * NT])
        qkv2 = sb("qkv2", [128, NT, 2])

        xnT = sb("xnT", [128, NTOK])
        gS = sb("gS", [3, NTOK])
        gsum = sb("gsum", [3, B * T])
        glin = sb("glin", [3, B * T])
        gates = sb("gates", [128, 3, B, TP])
        lrtok = sb("lrtok", [128, TP])
        qksq = sb("qksq", [128, NT, 2 * D])
        qkr = sb("qkr", [128, NT, 2])
        KK = sb("KK", [128, NT, 2 * D])
        QV = sb("QV", [128, NT, 2 * D])
        kk = sb("kk", [128, B, TP * C])
        qq = sb("qq", [128, NTOK])
        vT = sb("vT", [128, B, TP * C])
        kcur = [sb(f"kcur{n}", [128, B, 32]) for n in range(2)]
        vcur = [sb(f"vcur{n}", [128, B, C]) for n in range(2)]
        gcur = [sb(f"gcur{n}", [128, 3, B]) for n in range(2)]
        lrcur = [sb(f"lrcur{n}", [128, 1]) for n in range(2)]
        mem = sb("mem", [128, 5 * B * 2 * DE])

        def part(base, n, k):
            return mem[:, base:base + n * k].rearrange("p (n k) -> p n k", n=n)

        WB = B * 2 * DE
        P = part(0, B, 2 * DE)
        M = part(WB, B, 2 * DE)
        Me = part(2 * WB, B, 2 * DE)
        Pf = part(3 * WB, B, 2 * DE)
        Q = part(4 * WB, B, 2 * DE)
        w21T = sb("w21T", [128, B, DE])
        w20T = sb("w20T", [128, B, DE])
        w11T = sb("w11T", [128, B, D])
        g0T = sb("g0T", [128, B, C])
        g1T = sb("g1T", [128, B, C])
        h1T = sb("h1T", [128, B, 32])
        dT = sb("dT", [128, B, 32])
        dh1T = sb("dh1T", [128, B, 32])
        da1T = sb("da1T", [128, B, C])
        hv = sb("hv", [128, B, C])
        a0q, a0u, a0y, a0t, a0x, a0s = (sb(f"a0{c}", [128, DE]) for c in "quytxs")
        a1q, a1u, a1y, a1t, a1x, a1s = (sb(f"a1{c}", [128, DE]) for c in "quytxs")
        g0tok = sb("g0tok", [128, DE])
        h1tok = sb("h1tok", [128, D])
        g1tok = sb("g1tok", [128, DE])
        dtok = sb("dtok", [128, D])
        da1tok = sb("da1tok", [128, DE])
        dh1tok = sb("dh1tok", [128, D])
        da0tok = sb("da0tok", [128, DE])
        ktok = sb("ktok", [128, D])
        FW2 = sb("FW2", [128, 2, 2 * DE])
        FW = sb("FW", [128, 2 * DE])
        g0F = KK[:, :, :].rearrange("p n c -> p (n c)")
        g1F = QV[:, :, :].rearrange("p n c -> p (n c)")
        h1F = qksq[:, :, :].rearrange("p n c -> p (n c)")

        XT = KK
        x2A = sb("x2A", [128, NTOK])
        t1T = sb("t1T", [128, NTOK])
        L = sb("L", [128, NT, E])
        L2 = sb("L2", [128, NT, E])
        eq = sb("eq", [128, NT, E])
        cum = sb("cum", [128, NT, E])
        pick1 = sb("pick1", [128, NT, E])
        pick2 = sb("pick2", [128, NT, E])
        m1 = sb("m1", [128, NT])
        m2 = sb("m2", [128, NT])
        md = sb("md", [128, NT])
        p1 = sb("p1", [128, NT])
        p2 = sb("p2", [128, NT])
        W8 = sb("W8", [128, NT, E])
        W8T = sb("W8T", [E, NTOK])
        hT = sb("hT", [128, E, HC, NTOK // 2])
        yT = [sb(f"yT{n}", [128, NTOK // 2]) for n in range(2)]
        fold = sb("fold", [128, D])
        pick3 = sb("pick3", [128, E])
        halves = QV[:, :, :].rearrange("p n c -> p (n c)")
        W3 = halves[:, 0:NTOK // 2].bitcast(mybir.dt.bfloat16)
        sel = halves[:, NTOK // 2:NTOK].bitcast(mybir.dt.bfloat16)
        rest = KK[:, :, :].rearrange("p n c -> p (n c)")

        c1a = sb("c1a", [D + 1, D + 1])
        c1b = sb("c1b", [D + 1, D + 1])
        xcT = x2A[0:D + 1]
        img = [sb(f"img{n}", [128, PADW, PADW]) for n in range(2)]
        zim = [sb(f"zim{n}", [128, PADW, PADW]) for n in range(2)]
        rz = [sb(f"rz{n}", [128, S]) for n in range(2)]
        sc0 = sb("sc0", [128, NT, D + 1])
        b3n = sb("b3n", [128, 1])
        A3 = part(3 * WB - NT * D, NT, D)
        scanned = part(3 * WB, NT, D + 1)
        prod = part(4 * WB, NT, D + 1)

        t3T = part(0, S + 2 * LSTM_UN, B)[0:D + 1]
        hring = sb("hring", [D + 1, LSTM_UN, B])
        hist = part((S + 2 * LSTM_UN) * B, S + LSTM_UN, B)[0:D]
        lvh = sb("lvh", [D + 1, 3, D])
        gp = sb("gp", [D, B, 3])
        og = sb("og", [D, B])
        cs = [sb(f"cs{n}", [D, B, 3]) for n in range(2)]
        warm = sb("warm", [1, 2])
        idle = ctx.enter_context(nc.sbuf_tensor("idle", [128, 128 + FILL_N], mybir.dt.bfloat16))

        def inner(t):
            return t[:, 1:1 + W, 1:1 + W]

        block = ctx.enter_context(nc.Block())

        @block.sync
        def _(sp):
            sp.dma_start(xs[:, :, :], i_["x"]).then_inc(sem("ld_x"), 16)
            for dst, key, s in ((ident[:, :], "ident", "ld_id"), (wqkv[:, :], "wqkv", "ld_a"), (wgate[:, :], "wgate", "ld_a"),
                                (gaff[:, :], "gaff", "ld_g"), (gsel[:, :, :], "gsel", "ld_g"), (memw[:, :], "memw", "ld_m"),
                                (lng[:, :], "lng", "ld_w1"), (lnb[:, :], "lnb", "ld_w1"), (w1[:, :, :], "w1", "ld_w1"),
                                (w2[:, :, :, :], "w2", "ld_w2"), (b2[:, :], "b2", "ld_w2"),
                                (wr[D:128, :], "wr", "ld_r"), (br[:, :], "br", "ld_r"), (notfirst[:, :], "notfirst", "ld_r"),
                                (c1p[:, :, :], "c1p", "ld_c1"), (c1last[:, :], "c1last", "ld_c1"),
                                (w3[:, :], "w3", "ld_3"), (b3[:, :], "b3", "ld_3"), (cb2[:, :], "cb2", "ld_3"),
                                (lu[:, :, :], "lu", "ld_l"), (lv[:, :, :], "lv", "ld_l"),
                                (cw[:, :, :, :], "cw", "ld_cw")):
                sp.dma_start(dst, i_[key]).then_inc(sem(s), 16)
            sp.wait_ge(sem("x_done"), 1)
            sp.dma_start(out, xs[:, :, :]).then_inc(sem("stored"), 16)
            sp.wait_ge(sem("stored"), 16)

        @block.gpsimd
        def _(pool):
            nc.gpsimd.memset(idle[:, :], 0.0)
            nc.gpsimd.memset(xnT[:, :], 0.0).then_inc(sem("idle"), 1)
            for t in (*kcur, h1T, dT, dh1T):
                nc.gpsimd.memset(t[:, :, :], 0.0)
            nc.gpsimd.memset(M[:, :, :], 0.0)
            nc.gpsimd.memset(gates[:, :, :, :], 0.0)
            nc.gpsimd.memset(lrtok[:, :], 0.0)
            nc.gpsimd.memset(kk[:, :, S:], 0.0)
            nc.gpsimd.memset(vT[:, :, S:], 0.0)
            nc.gpsimd.memset(sc0[:, :, :], 0.0)
            nc.gpsimd.memset(gp[:, :, :], 0.0)
            for t in (*img, *zim):
                nc.gpsimd.memset(t[:, :, :], 0.0)
            nc.gpsimd.memset(qq[:, :], 0.0)
            nc.gpsimd.memset(warm[:, :], 0.0).then_inc(sem("cleared"), 1)

            def prefetch(t, n):
                nc.gpsimd.tensor_copy(kcur[n][:, :, 0:C], kview(kk, t))
                nc.gpsimd.tensor_copy(vcur[n][:, :, :], kview(vT, t))
                nc.gpsimd.tensor_copy(gcur[n][:, :, :], gates[:, :, :, bass.ds(t, 1)].rearrange("p g b o -> p g (b o)"))
                nc.gpsimd.tensor_copy(lrcur[n][:, :], lrtok[:, bass.ds(t, 1)]).then_inc(sem("pre"), 1)

            def kview(tile, t, lo=0):
                return tile[lo:128, :, bass.ds(t * C, C)]

            pool.wait_ge(sem("cleared"), 1)
            pool.wait_ge(sem("gates"), 5)
            pool.wait_ge(sem("kkT_a"), 2)
            pool.wait_ge(sem("kkT_v"), 2)
            prefetch(0, 0)
            with nc.gpsimd.Fori(0, T, MEM_UN) as i:
                for u in range(MEM_UN):
                    t = i + u
                    n = u % 2
                    pool.wait_ge(sem("pre"), t + 1)
                    pool.wait_ge(sem("m_new"), t + 1)
                    nc.gpsimd.tensor_tensor(Me[:, :, :], M[:, :, :], wide(gcur[n][:, 0, :], 2 * DE), ALU.mult)
                    nc.gpsimd.tensor_tensor(Pf[:, :, :], P[:, :, :], wide(gcur[n][:, 1, :], 2 * DE),
                                            ALU.mult).then_inc(sem("decayed"), 1)
                    pool.wait_ge(sem("decayed"), t + 1)
                    nc.gpsimd.tensor_tensor(Q[:, :, :], Pf[:, :, :], Me[:, :, :], ALU.add).then_inc(sem("Q"), 1)
                    prefetch(t + 1, 1 - n)

            pool.wait_ge(sem("pre"), T + 1)
            nc.gpsimd.memset(h1F[0:D, :], 0.0).then_inc(sem("h1F_zeros"), 1)
            nc.gpsimd.memset(w1g[:, :, :], 0.0)
            nc.gpsimd.memset(x2A[:, :], 0.0).then_inc(sem("zeros"), 1)
            pool.wait_ge(sem("zeros"), 1)
            pool.wait_ge(sem("ld_w1"), 48)
            nc.gpsimd.tensor_tensor(w1g[0:D, :, :], w1[0:D, :, :], wide(lng[:, :], H), ALU.mult).then_inc(sem("w1g"), 1)

            pool.wait_ge(sem("f_y"), 2)
            pool.wait_ge(sem("w1g"), 1)
            nc.gpsimd.memset(W3, 0.0).then_inc(sem("zeros3"), 1)

            HU = LSTM_UN // 2
            nc.gpsimd.memset(hring[:, :, :], 0.0).then_inc(sem("h_saved"), HU + 1)
            with nc.gpsimd.Fori(0, S, LSTM_UN) as i:
                for u in (0, HU):
                    pool.wait_ge(sem("h_new"), i + (u + HU + 1))
                    nc.gpsimd.tensor_copy(hist[:, bass.ds(i + u, HU), :], hring[0:D, u:u + HU, :]).then_inc(sem("h_saved"), HU)

        @block.tensor
        def _(pe):
            up = ident[64:128, 64:128]

            def busy(count, bank):
                for _ in range(count):
                    nc.tensor.matmul(bk[:, bank, 0:512], idle[:, 0:128], idle[:, 128:128 + 512], start=True, stop=True)

            def keep_busy(place, bank):
                for _ in range(BUSY[place]):
                    nc.tensor.matmul(bk[:, bank, 0:256], idle[:, 0:128], idle[:, 128:128 + 256], start=True, stop=True)

            pe.wait_ge(sem("idle"), 1)
            busy(AFTER[2], 7)
            pe.wait_ge(sem("ld_id"), 16)
            pe.wait_ge(sem("ln"), 1)
            for n in range(NT):
                ins = nc.tensor.transpose(bk[0:D, n // 4, (n % 4) * 128:(n % 4 + 1) * 128], xn[:, n, :], ident[:, :])
                if n % 4 == 3:
                    ins.then_inc(sem("xnT_ps"), 1)
            pe.wait_ge(sem("ld_a"), 32)
            pe.wait_ge(sem("xnT"), 2)
            for n in range(NT):
                ins = nc.tensor.matmul(bk[:, 4 + n // 2, (n % 2) * 192:(n % 2 + 1) * 192],
                                       xnT[:, n * 128:(n + 1) * 128], wqkv[:, :], start=True, stop=True)
                if n % 2 == 1:
                    ins.then_inc(sem("qkv_ps"), 1)
            for n in range(2):
                nc.tensor.matmul(bk[0:3, 2 + n, :], wgate[:, :], xnT[:, n * 512:(n + 1) * 512], start=True,
                                 stop=True).then_inc(sem("glog"), 1)
            busy(AFTER[3], 0)
            pe.wait_ge(sem("KK"), 1)
            for n in range(NT):
                ins = nc.tensor.transpose(bk[:, n // 4, (n % 4) * 128:(n % 4 + 1) * 128], KK[:, n, :], ident[:, :])
            ins.then_inc(sem("kkT_ps"), 1)
            pe.wait_ge(sem("QV"), 2)
            for n in range(NT):
                ins = nc.tensor.transpose(bk[:, 4 + n // 4, (n % 4) * 128:(n % 4 + 1) * 128], QV[:, n, :], ident[:, :])
            ins.then_inc(sem("qvT_ps"), 1)
            pe.wait_ge(sem("ld_g"), 32)
            pe.wait_ge(sem("glin"), 1)
            for g in range(3):
                ins = nc.tensor.matmul(bk[:, 2, g * B * T:(g + 1) * B * T], gsel[:, g, :], glin[:, :], start=True, stop=True)
            ins.then_inc(sem("gate_ps"), 1)
            busy(AFTER[4], 6)
            pe.wait_ge(sem("ps_clear"), 1)

            with nc.tensor.Fori(0, T, MEM_UN) as i:
                for u in range(MEM_UN):
                    t1 = i + (u + 1)
                    kc = kcur[u % 2]
                    pe.wait_ge(sem("pre"), t1)
                    keep_busy(0, 0)
                    pe.wait_ge(sem("ld_id"), 16)
                    pe.wait_ge(sem("p1_new"), t1)
                    for b in range(B):
                        ins = nc.tensor.matmul(bk[32 * b:32 * b + C, 1, 0:DE], kc[0:D, b, 0:C], P[0:D, b, 0:DE],
                                               start=True, stop=True)
                    ins.then_inc(sem("a0tok"), 1)
                    nc.tensor.transpose(bk[:, 2, 448:448 + D], kc[0:D, :, :].rearrange("p b c -> p (b c)"),
                                        ident[0:D, 0:D]).then_inc(sem("ktok_ps"), 1)
                    keep_busy(1, 0)
                    pe.wait_ge(sem("g0tok"), t1)
                    nc.tensor.transpose(bk[:, 0, 0:128], g0tok[:, :], ident[:, :]).then_inc(sem("g0T_ps"), 1)
                    for b in range(B):
                        ins = nc.tensor.transpose(bk[:, 3, 256 + b * D:256 + (b + 1) * D], P[D:128, b, 0:DE], up)
                    ins.then_inc(sem("w11T_ps"), 1)
                    pe.wait_ge(sem("g0T"), t1)
                    pe.wait_ge(sem("p2_new"), t1)
                    for b in range(B):
                        ins = nc.tensor.matmul(bk[64:128, 2, b * C:(b + 1) * C], P[:, b, DE:DE + D], g0T[:, b, :],
                                               start=True, stop=True)
                    ins.then_inc(sem("h1_ps"), 1)
                    pe.wait_ge(sem("ld_id"), 16)
                    pe.wait_ge(sem("m_new"), t1)
                    for b in range(B):
                        ins = nc.tensor.transpose(bk[0:D, 4, b * DE:(b + 1) * DE], P[:, b, DE + D:2 * DE], ident[:, :])
                    ins.then_inc(sem("w21T_ps"), 1)
                    keep_busy(3, 7)
                    pe.wait_ge(sem("ld_id"), 16)
                    pe.wait_ge(sem("w11T"), t1)
                    pe.wait_ge(sem("h1T"), t1)
                    for b in range(B):
                        ins = nc.tensor.matmul(bk[32 * b:32 * b + C, 3, 0:DE], h1T[64:128, b, 0:C], P[D:128, b, 0:DE],
                                               start=True, stop=True)
                    ins.then_inc(sem("a1tok"), 1)
                    nc.tensor.transpose(bk[:, 0, 128:128 + D], h1T[64:128, :, :].rearrange("p b c -> p (b c)"),
                                        up).then_inc(sem("h1tok_ps"), 1)
                    keep_busy(4, 7)
                    pe.wait_ge(sem("g1tok"), t1)
                    nc.tensor.transpose(bk[:, 1, 128:256], g1tok[:, :], ident[:, :]).then_inc(sem("g1T_ps"), 1)
                    for b in range(B):
                        ins = nc.tensor.transpose(bk[0:D, 6, b * DE:(b + 1) * DE], P[:, b, DE:DE + D], ident[:, :])
                    ins.then_inc(sem("w20T_ps"), 1)
                    keep_busy(5, 7)
                    pe.wait_ge(sem("g1T"), t1)
                    for b in range(B):
                        ins = nc.tensor.matmul(bk[64:128, 2, 64 + b * C:64 + (b + 1) * C], P[:, b, DE + D:2 * DE],
                                               g1T[:, b, :], start=True, stop=True)
                    ins.then_inc(sem("pred_ps"), 1)
                    keep_busy(6, 7)
                    pe.wait_ge(sem("ld_id"), 16)
                    pe.wait_ge(sem("w21T"), t1)
                    pe.wait_ge(sem("h1tok"), t1)
                    pe.wait_ge(sem("dT"), t1)
                    for b in range(B):
                        ins = nc.tensor.matmul(bk[32 * b:32 * b + C, 2, 128:128 + DE], dT[64:128, b, 0:C], w21T[64:128, b, :],
                                               start=True, stop=True)
                    ins.then_inc(sem("dg1_ps"), 1)
                    nc.tensor.transpose(bk[:, 0, 192:192 + D], dT[64:128, :, :].rearrange("p b c -> p (b c)"),
                                        up).then_inc(sem("dtok_ps"), 1)
                    keep_busy(7, 7)
                    pe.wait_ge(sem("w20T"), t1)
                    pe.wait_ge(sem("dtok"), t1)

                    def grad21(b):
                        r = slice(32 * b, 32 * b + C)
                        nc.tensor.matmul(bk[:, 4 + b, 192:256], g1tok[r, :], dtok[r, :], start=True, stop=True)

                    grad21(0)
                    pe.wait_ge(sem("da1tok"), t1)
                    nc.tensor.transpose(bk[:, 1, 256:384], da1tok[:, :], ident[:, :]).then_inc(sem("da1T_ps"), 1)
                    grad21(1)
                    grad21(2)
                    keep_busy(9, 3)
                    pe.wait_ge(sem("da1T"), t1)
                    for b in range(B):
                        ins = nc.tensor.matmul(bk[64:128, 2, 256 + b * C:256 + (b + 1) * C], w11T[:, b, :],
                                               da1T[:, b, :], start=True, stop=True)
                    ins.then_inc(sem("dh1_ps"), 1)
                    grad21(3)
                    keep_busy(10, 3)
                    pe.wait_ge(sem("ld_id"), 16)
                    pe.wait_ge(sem("w20T"), t1)
                    pe.wait_ge(sem("dh1T"), t1)
                    nc.tensor.transpose(bk[:, 0, 256:256 + D], dh1T[64:128, :, :].rearrange("p b c -> p (b c)"),
                                        up).then_inc(sem("dh1tok_ps"), 1)
                    for b in range(B):
                        ins = nc.tensor.matmul(bk[32 * b:32 * b + C, 2, 320:320 + DE], dh1T[64:128, b, 0:C],
                                               w20T[64:128, b, :], start=True, stop=True)
                    ins.then_inc(sem("dg0_ps"), 1)
                    keep_busy(8, 3)
                    pe.wait_ge(sem("dh1tok"), t1)
                    for b in range(B):
                        r = slice(32 * b, 32 * b + C)
                        nc.tensor.matmul(bk[:, 4 + b, 128:192], g0tok[r, :], dh1tok[r, :], start=True, stop=True)
                    keep_busy(11, 3)
                    pe.wait_ge(sem("da0tok"), t1)
                    for b in range(B):
                        r = slice(32 * b, 32 * b + C)
                        nc.tensor.matmul(bk[64:128, 4 + b, 0:DE], h1tok[r, :], da1tok[r, :], start=True, stop=True)
                        ins = nc.tensor.matmul(bk[0:D, 4 + b, 0:DE], ktok[r, :], da0tok[r, :], start=True, stop=True)
                    ins.then_inc(sem("grads"), 1)

            pe.wait_ge(sem("p2_new"), T + 1)
            busy(AFTER[0], 0)
            pe.wait_ge(sem("qq"), 2)
            pe.wait_ge(sem("FW"), 1)
            for n in range(2):
                nc.tensor.matmul(bk[:, 2 + n, :], FW[:, 0:DE], qq[:, n * 512:(n + 1) * 512], start=True,
                                 stop=True).then_inc(sem("f_a0"), 1)
            for n in range(2):
                pe.wait_ge(sem("f_g0"), n + 1)
                nc.tensor.matmul(bk[64:128, 4 + n, :], FW[:, DE:DE + D], g0F[:, n * 512:(n + 1) * 512], start=True,
                                 stop=True).then_inc(sem("f_h1_ps"), 1)
            pe.wait_ge(sem("h1F_zeros"), 1)
            for n in range(2):
                pe.wait_ge(sem("f_h1"), n + 1)
                nc.tensor.matmul(bk[:, 6 + n, :], FW[:, 0:DE], h1F[:, n * 512:(n + 1) * 512], start=True,
                                 stop=True).then_inc(sem("f_a1"), 1)
            for n in range(NT):
                if n % 4 == 0:
                    pe.wait_ge(sem("f_g1"), n // 4 + 1)
                nc.tensor.matmul(bk[:, n // 4, (n % 4) * D:(n % 4 + 1) * D], g1F[:, n * 128:(n + 1) * 128], FW[:, DE + D:2 * DE],
                                 start=True, stop=False)
                ins = nc.tensor.matmul(bk[:, n // 4, (n % 4) * D:(n % 4 + 1) * D], h1F[:, n * 128:(n + 1) * 128], ident[:, 64:128],
                                       start=False, stop=True)
                if n % 4 == 3:
                    ins.then_inc(sem("f_y"), 1)

            pe.wait_ge(sem("ld_c1"), 32)
            nc.tensor.matmul(bk[0:D + 1, 2, 0:D + 1], c1p[:, 2, :], c1last[:, :], start=True, stop=True).then_inc(sem("c1_ps"), 1)
            pe.wait_ge(sem("ld_w1"), 48)
            for e in range(E):
                ins = nc.tensor.matmul(bk[64:65, 4 + e // 2, (e % 2) * H:(e % 2 + 1) * H], lnb[:, e:e + 1], w1[:, e, :],
                                       start=True, stop=True)
            ins.then_inc(sem("w1row_ps"), 1)
            pe.wait_ge(sem("c1"), 1)
            nc.tensor.matmul(bk[0:D + 1, 3, 0:D + 1], c1p[:, 1, :], c1a[:, :], start=True, stop=True).then_inc(sem("c1_ps"), 1)
            pe.wait_ge(sem("c1"), 2)
            nc.tensor.matmul(bk[0:D + 1, 2, 0:D + 1], c1p[:, 0, :], c1b[:, :], start=True, stop=True).then_inc(sem("c1_ps"), 1)
            pe.wait_ge(sem("c1"), 3)
            busy(AFTER[1], 7)

            pe.wait_ge(sem("XT"), 1)
            for n in range(NT):
                ins = nc.tensor.transpose(bk[:, 2 + n // 4, (n % 4) * 128:(n % 4 + 1) * 128], XT[:, n, :], ident[:, :])
                if n % 4 == 3:
                    ins.then_inc(sem("XT_ps"), 1)
            pe.wait_ge(sem("ld_r"), 48)
            pe.wait_ge(sem("t1T"), 2)
            for n in range(NT):
                ins = nc.tensor.matmul(bk[:, 0, n * E:(n + 1) * E], t1T[64:128, n * 128:(n + 1) * 128], wr[64:128, :],
                                       start=True, stop=True)
            ins.then_inc(sem("logit_ps"), 1)
            pe.wait_ge(sem("x2A"), 3)
            pe.wait_ge(sem("ld_w2"), 32)

            def up_proj(g):
                for c in range(HC):
                    k = g * HC + c
                    if k >= 4:
                        pe.wait_ge(sem("hT"), k - 3)
                    nc.tensor.matmul(bk[:, 4 + k % 4, :], w1g[:, g % E, c * 128:(c + 1) * 128],
                                     x2A[:, g // E * 512:(g // E + 1) * 512], start=True, stop=True).then_inc(sem("hid_ps"), 1)

            def spread(g):
                if g >= 2:
                    pe.wait_ge(sem("hw"), g - 1)
                nc.tensor.matmul(bk[:, g % 2, :], sel[:, g % E * 128:(g % E + 1) * 128], W3[:, g // E * 512:(g // E + 1) * 512],
                                 start=True, stop=True).then_inc(sem("spread"), 1)

            def down_proj(g):
                hf, e = g // E, g % E
                if e == 0:
                    nc.tensor.matmul(bk[0:D, 2 + hf, :], b2[:, :], W8T[:, hf * 512:(hf + 1) * 512], start=True, stop=False,
                                     skip_group_check=True)
                pe.wait_ge(sem("hw"), g + 1)
                for c in range(HC):
                    ins = nc.tensor.matmul(bk[c * D:(c + 1) * D, 2 + hf, :], w2[:, e, c, :], hT[:, e, c, :],
                                           start=(e == 0 and c == 1), stop=(e == E - 1), skip_group_check=True)
                ins.then_inc(sem("down"), 1)

            def back(hf):
                pe.wait_ge(sem("yT"), hf + 1)
                for j in range(4):
                    ins = nc.tensor.matmul(bk[:, 2 + hf, j * D:(j + 1) * D], yT[hf][:, j * 128:(j + 1) * 128], fold[:, :],
                                           start=True, stop=True)
                ins.then_inc(sem("back"), 1)

            pe.wait_ge(sem("w1row"), 1)
            for g in range(3):
                up_proj(g)
            pe.wait_ge(sem("W8"), 1)
            for n in range(NT):
                ins = nc.tensor.transpose(bk[0:E, n // 4, (n % 4) * 128:(n % 4 + 1) * 128], W8[:, n, :], ident[:, :])
            ins.then_inc(sem("W8T_ps"), 1)
            for g in range(3, LEAD):
                up_proj(g)
            pe.wait_ge(sem("sel"), 1)
            pe.wait_ge(sem("W8T"), 2)
            for g in range(2 * E):
                if g % E == 0:
                    pe.wait_ge(sem("W3"), g // E + 1)
                spread(g)
                if g + LEAD < 2 * E:
                    up_proj(g + LEAD)
                if g >= 1:
                    down_proj(g - 1)
                if g == E + 2:
                    back(0)
            down_proj(2 * E - 1)
            back(1)

            busy(AFTER[5], 0)
            pe.wait_ge(sem("ln"), 2)
            for n in range(NT):
                ins = nc.tensor.transpose(bk[0:D, 4 + n // 4, (n % 4) * 128:(n % 4 + 1) * 128], xn[:, n, :], ident[:, :])
                if n % 4 == 3:
                    ins.then_inc(sem("xcT_ps"), 1)
            pe.wait_ge(sem("xcT"), 2)
            for g in range(2):
                for q in range(B):
                    ins = nc.tensor.matmul(bk[32 * q:32 * q + 32, 2 + g, 0:S], c1a[:, 32 * g:32 * g + 32],
                                           xcT[:, q * S:(q + 1) * S], start=True, stop=True)
                ins.then_inc(sem("c1out"), 1)

            def taps(bank, kind, src, first, last):
                for k in range(9):
                    ins = nc.tensor.matmul(bk[:, bank, 0:S], cw[:, kind, k, :], src[:, k // 3:k // 3 + W, k % 3:k % 3 + W],
                                           start=(first and k == 0), stop=(last and k == 8), skip_group_check=True)
                return ins

            busy(AFTER[6], 0)
            pe.wait_ge(sem("ld_cw"), 16)
            pe.wait_ge(sem("img"), 2)
            taps(0, 0, img[0], True, False)
            taps(0, 1, img[1], False, True).then_inc(sem("z_ps"), 1)
            taps(1, 3, img[1], True, False)
            pe.wait_ge(sem("z"), 1)
            taps(0, 2, zim[0], False, True).then_inc(sem("z_ps"), 1)
            pe.wait_ge(sem("z"), 2)
            taps(1, 4, zim[0], False, True).then_inc(sem("z_ps"), 1)
            pe.wait_ge(sem("z"), 3)
            taps(1, 5, zim[1], False, True).then_inc(sem("z_ps"), 1)
            for g in range(2):
                pe.wait_ge(sem("rz"), g + 1)
                for c in range(2):
                    ins = nc.tensor.transpose(bk[:, 2 + g, c * 128:(c + 1) * 128], rz[g][:, c * 128:(c + 1) * 128], ident[:, :])
                ins.then_inc(sem("A3_ps"), 1)

            busy(AFTER[7], 0)
            pe.wait_ge(sem("ln"), 3)
            for n in range(NT):
                ins = nc.tensor.transpose(bk[0:D, 4 + n // 4, (n % 4) * 128:(n % 4 + 1) * 128], xn[:, n, :], ident[:, :])
                if n % 4 == 3:
                    ins.then_inc(sem("t3T_ps"), 1)
            pe.wait_ge(sem("ld_l"), 32)
            pe.wait_ge(sem("t3T"), 3)
            HU = LSTM_UN // 2

            def inputs_part(par, t):
                for g in range(3):
                    nc.tensor.matmul(bk[0:D, 3 * par + g, 0:HU * B], lu[:, g, :], t3T[:, bass.ds(t, HU), :] if not isinstance(t, int)
                                     else t3T[:, t:t + HU, :], start=True, stop=False, skip_group_check=True)

            inputs_part(0, 0)
            pe.wait_ge(sem("h_saved"), HU + 1)
            with nc.tensor.Fori(0, S, LSTM_UN) as i:
                for u in range(LSTM_UN):
                    for _ in range(FILL):
                        nc.tensor.matmul(bk[:, 7, 0:FILL_N], idle[:, 0:128], idle[:, 128:128 + FILL_N], start=True, stop=True)
                    pe.wait_ge(sem("h_new"), i + (u + 1))
                    for g in range(3):
                        nc.tensor.matmul(bk[0:D, 3 * (u // HU) + g, (u % HU) * B:(u % HU + 1) * B], lvh[:, g, :],
                                         hring[:, (u - 1) % LSTM_UN, :], start=False, stop=True,
                                         skip_group_check=True).then_inc(sem(f"gate{g}_ps"), 1)
                    if u == 1:
                        inputs_part(1, i + HU)
                    if u == HU + 1:
                        inputs_part(0, i + 2 * HU)
            pe.wait_ge(sem("h_saved"), S + HU + 1)
            for n in range(NT):
                b, c = n // 2, n % 2
                ins = nc.tensor.transpose(bk[:, 7, n * D:(n + 1) * D], hist[:, c * 128:(c + 1) * 128, b], ident[0:D, 0:D])
            ins.then_inc(sem("hs_ps"), 1)

        @block.scalar
        def _(act):
            def table(f):
                nc.scalar.activation(warm[:, 0:1], warm[:, 1:2], f)

            def root(n):
                act.wait_ge(sem("var"), n)
                nc.scalar.activation(sd[:, :], rs[:, :], ACT.Sqrt).then_inc(sem("std"), 1)

            act.wait_ge(sem("cleared"), 1)
            table(ACT.Sqrt)
            root(1)
            for n in range(2):
                act.wait_ge(sem("xnT_ps"), n + 1)
                nc.scalar.copy(xnT[0:D, n * 512:(n + 1) * 512], bk[0:D, n, :]).then_inc(sem("xnT"), 1)
            act.wait_ge(sem("qkv_ps"), 4)
            qkv = bk[:, 4:8, 0:384].rearrange("p k (n c) -> p k n c", n=2)
            nc.scalar.activation(qksq[:, :, :].rearrange("p (k n) c -> p k n c", n=2), qkv[:, :, :, 0:2 * D],
                                 ACT.Square).then_inc(sem("qksq"), 1)
            nc.scalar.copy(QV[:, :, D:2 * D].rearrange("p (k n) c -> p k n c", n=2), qkv[:, :, :, 2 * D:3 * D]).then_inc(sem("QV"), 1)
            act.wait_ge(sem("qk_sq"), 1)
            nc.scalar.activation(qkr[:, :, :], qkv2[:, :, :], ACT.Sqrt).then_inc(sem("qk_n"), 1)
            table(ACT.Gelu_apprx_tanh)
            for n in range(2):
                act.wait_ge(sem("glog"), n + 1)
                nc.scalar.activation(gS[:, n * 512:(n + 1) * 512], bk[0:3, 2 + n, :], ACT.Tanh, scale=0.5).then_inc(sem("gS"), 1)
            act.wait_ge(sem("kkT_ps"), 1)
            nc.scalar.copy(kk[:, 0:2, 0:S], bk[:, 0, :].rearrange("p (b s) -> p b s", b=2)).then_inc(sem("kkT_a"), 1)
            act.wait_ge(sem("qvT_ps"), 1)
            nc.scalar.copy(vT[:, 0:2, 0:S], bk[:, 4, :].rearrange("p (b s) -> p b s", b=2)).then_inc(sem("kkT_a"), 1)
            nc.scalar.copy(qq[0:D, 0:512], bk[0:D, 4, :]).then_inc(sem("qq"), 1)

            def tokens(t):
                return t.rearrange("p (b c) -> p b c", b=B)[:, :, 0:C]

            with nc.scalar.Fori(0, T, MEM_UN) as i:
                for u in range(MEM_UN):
                    t1 = i + (u + 1)
                    lr = lrcur[u % 2][:, 0:1]
                    act.wait_ge(sem("a0tok"), t1)
                    nc.scalar.activation(g0tok[:, :], bk[:, 1, 0:DE], ACT.Gelu_apprx_tanh).then_inc(sem("g0tok"), 1)
                    nc.scalar.activation(a0q[:, :], bk[:, 1, 0:DE], ACT.Square).then_inc(sem("a0q"), 1)
                    act.wait_ge(sem("ktok_ps"), t1)
                    nc.scalar.activation(ktok[:, :], bk[:, 2, 448:448 + D], ACT.Copy, scale=lr).then_inc(sem("ktok"), 1)
                    act.wait_ge(sem("g0T_ps"), t1)
                    nc.scalar.copy(g0T[:, :, :], tokens(bk[:, 0, 0:128])).then_inc(sem("g0T"), 1)
                    act.wait_ge(sem("w11T_ps"), t1)
                    nc.scalar.copy(w11T[:, :, :].rearrange("p b e -> p (b e)"), bk[:, 3, 256:512]).then_inc(sem("w11T"), 1)
                    act.wait_ge(sem("a0u"), t1)
                    nc.scalar.activation(a0t[:, :], a0u[:, :], ACT.Tanh, scale=RT2PI * KAPPA).then_inc(sem("a0t"), 1)
                    act.wait_ge(sem("a0t"), t1)
                    nc.scalar.activation(a0s[:, :], a0t[:, :], ACT.Square).then_inc(sem("a0tq"), 1)
                    act.wait_ge(sem("w21T_ps"), t1)
                    nc.scalar.mul(w21T[64:128, :, :].rearrange("p b e -> p (b e)"), bk[0:D, 4, :], 0.5).then_inc(sem("w21T"), 1)
                    act.wait_ge(sem("a1tok"), t1)
                    nc.scalar.activation(g1tok[:, :], bk[:, 3, 0:DE], ACT.Gelu_apprx_tanh).then_inc(sem("g1tok"), 1)
                    nc.scalar.activation(a1q[:, :], bk[:, 3, 0:DE], ACT.Square).then_inc(sem("a1q"), 1)
                    act.wait_ge(sem("g1T_ps"), t1)
                    nc.scalar.copy(g1T[:, :, :], tokens(bk[:, 1, 128:256])).then_inc(sem("g1T"), 1)
                    act.wait_ge(sem("h1tok_ps"), t1)
                    nc.scalar.activation(h1tok[:, :], bk[:, 0, 128:128 + D], ACT.Copy, scale=lr).then_inc(sem("h1tok"), 1)
                    act.wait_ge(sem("a1u"), t1)
                    nc.scalar.activation(a1t[:, :], a1u[:, :], ACT.Tanh, scale=RT2PI * KAPPA).then_inc(sem("a1t"), 1)
                    act.wait_ge(sem("a1t"), t1)
                    nc.scalar.activation(a1s[:, :], a1t[:, :], ACT.Square).then_inc(sem("a1tq"), 1)
                    act.wait_ge(sem("w20T_ps"), t1)
                    nc.scalar.mul(w20T[64:128, :, :].rearrange("p b e -> p (b e)"), bk[0:D, 6, :], 0.5).then_inc(sem("w20T"), 1)
                    act.wait_ge(sem("dtok_ps"), t1)
                    nc.scalar.activation(dtok[:, :], bk[:, 0, 192:192 + D], ACT.Copy, scale=lr).then_inc(sem("dtok"), 1)
                    act.wait_ge(sem("da1T_ps"), t1)
                    nc.scalar.copy(da1T[:, :, :], tokens(bk[:, 1, 256:384])).then_inc(sem("da1T"), 1)
                    act.wait_ge(sem("dh1tok_ps"), t1)
                    nc.scalar.activation(dh1tok[:, :], bk[:, 0, 256:256 + D], ACT.Copy, scale=lr).then_inc(sem("dh1tok"), 1)

            for n in range(2):
                act.wait_ge(sem("f_a0"), n + 1)
                nc.scalar.activation(g0F[:, n * 512:(n + 1) * 512], bk[:, 2 + n, :], ACT.Gelu_apprx_tanh).then_inc(sem("f_g0"), 1)
            for n in range(2):
                act.wait_ge(sem("f_a1"), n + 1)
                nc.scalar.activation(g1F[:, n * 512:(n + 1) * 512], bk[:, 6 + n, :], ACT.Gelu_apprx_tanh).then_inc(sem("f_g1"), 1)
            table(ACT.Sqrt)
            for k, dst in enumerate((c1a, c1b, c1a)):
                act.wait_ge(sem("c1_ps"), k + 1)
                nc.scalar.copy(dst[:, :], bk[0:D + 1, 2 + k % 2, 0:D + 1]).then_inc(sem("c1"), 1)
                if k == 0:
                    act.wait_ge(sem("w1row_ps"), 1)
                    act.wait_ge(sem("w1g"), 1)
                    nc.scalar.copy(w1g[D:D + 1, :, :].rearrange("p (k n) h -> p k (n h)", k=4), bk[64:65, 4:8, :]).then_inc(sem("w1row"), 1)
            root(2)
            root(3)
            table(ACT.Gelu)

            for n in range(2):
                act.wait_ge(sem("XT_ps"), n + 1)
                nc.scalar.copy(x2A[0:D, n * 512:(n + 1) * 512], bk[0:D, 2 + n, :]).then_inc(sem("x2A"), 1)

            def gelus(g):
                if g >= E:
                    act.wait_ge(sem("down"), g - E + 1)
                for c in range(HC):
                    act.wait_ge(sem("hid_ps"), g * HC + c + 1)
                    nc.scalar.activation(hT[:, g % E, c, :], bk[:, 4 + (g * HC + c) % 4, :], ACT.Gelu).then_inc(sem("hT"), 1)

            act.wait_ge(sem("md"), 1)
            nc.scalar.activation(p1[:, :], md[:, :], ACT.Tanh, scale=0.5).then_inc(sem("p12"), 1)
            for g in range(3):
                gelus(g)
            act.wait_ge(sem("W8T_ps"), 1)
            for n in range(2):
                nc.scalar.copy(W8T[:, n * 512:(n + 1) * 512], bk[0:E, n, :]).then_inc(sem("W8T"), 1)
            for g in range(3, 2 * E):
                gelus(g)

            table(ACT.Sqrt)
            root(4)
            for n in range(2):
                act.wait_ge(sem("xcT_ps"), n + 1)
                nc.scalar.copy(xcT[0:D, n * 512:(n + 1) * 512], bk[0:D, 4 + n, :]).then_inc(sem("xcT"), 1)
            for g in range(2):
                act.wait_ge(sem("c1out"), g + 1)
                nc.scalar.activation(inner(img[g]), bk[:, 2 + g, 0:S].rearrange("p (y x) -> p y x", x=W), ACT.Relu).then_inc(sem("img"), 1)
            act.wait_ge(sem("ld_3"), 48)
            act.wait_ge(sem("z"), 2)
            nc.scalar.activation(rz[0][:, :], bk[:, 0, 0:S], ACT.Relu, bias=cb2[:, 0:1]).then_inc(sem("rz"), 1)
            act.wait_ge(sem("z_ps"), 4)
            nc.scalar.activation(rz[1][:, :], bk[:, 1, 0:S], ACT.Relu, bias=cb2[:, 0:1]).then_inc(sem("rz"), 1)

            root(5)
            table(ACT.Tanh)
            act.wait_ge(sem("rec_init"), 1)
            HU = LSTM_UN // 2
            with nc.scalar.Fori(0, S, LSTM_UN) as i:
                for u in range(LSTM_UN):
                    t1 = i + (u + 1)
                    cols = slice((u % HU) * B, (u % HU + 1) * B)
                    bank = 3 * (u // HU)
                    act.wait_ge(sem("gate0_ps"), t1)
                    nc.scalar.activation(gp[:, :, 0:2], wide(bk[0:D, bank, cols], 2), ACT.Tanh)
                    act.wait_ge(sem("gate1_ps"), t1)
                    nc.scalar.activation(bk[0:D, 6, 1:3 * B:3], bk[0:D, bank + 1, cols], ACT.Tanh, scale=0.5).then_inc(sem("in_gate"), 1)
                    act.wait_ge(sem("gate2_ps"), t1)
                    nc.scalar.activation(og[:, :], bk[0:D, bank + 2, cols], ACT.Tanh, scale=0.5)
                    act.wait_ge(sem("c_new"), t1)
                    nc.scalar.activation(bk[0:D, 6, 16:16 + B], cs[u % 2][:, :, 2], ACT.Tanh, scale=0.5).then_inc(sem("tanh_c"), 1)

        @block.vector
        def _(dve):
            links, norms = [0], [0]

            def link(ins):
                links[0] += 1
                ins.then_inc(sem("dve"), 1)
                dve.wait_ge(sem("dve"), links[0])

            def newton(y, v, tmp):
                link(nc.vector.tensor_tensor(tmp, y, y, ALU.mult))
                link(nc.vector.scalar_tensor_tensor(tmp, tmp, -0.5, v, ALU.mult, ALU.mult))
                link(nc.vector.scalar_tensor_tensor(y, tmp, 1.5, y, ALU.add, ALU.mult))

            def rstd():
                norms[0] += 1
                dve.wait_ge(sem("std"), norms[0])
                link(nc.vector.reciprocal(sd[:, :], sd[:, :]))
                newton(sd[:, :], rs[:, :], nt[:, 0:NT])

            def norm(src, dst, eps, signal):
                for n in range(NT):
                    ins = nc.vector.bn_stats(bst[:, n, :], src[:, n, :])
                link(ins)
                for n in range(NT):
                    ins = nc.vector.bn_aggr(mv[:, n, :], bst[:, n, :])
                link(ins)
                nc.vector.tensor_scalar(rs[:, :], mv[:, :, 1], eps, None, ALU.add).then_inc(sem("var"), 1)
                nc.vector.tensor_tensor(xc[:, :, :], src, wide(mv[:, :, 0], D), ALU.subtract)
                rstd()
                ins = nc.vector.tensor_tensor(dst, xc[:, :, :], wide(sd[:, :], D), ALU.mult)
                if signal:
                    ins.then_inc(sem(signal), 1)
                return ins

            dve.wait_ge(sem("ld_x"), 16)
            norm(xs[:, :, :], xn[:, :, :], 1e-6, "ln")
            dve.wait_ge(sem("ld_m"), 16)
            nc.vector.tensor_copy(P[:, :, :], mid(memw[:, :], B)).then_inc(sem("p1_new"), 1)
            dve.wait_ge(sem("qksq"), 1)
            link(nc.vector.tensor_reduce(qkr[:, :, :], qksq[:, :, :].rearrange("p n (a c) -> p n a c", a=2), AX, ALU.add))
            nc.vector.tensor_scalar(qkv2[:, :, :], qkr[:, :, :], 1e-24, None, ALU.max).then_inc(sem("qk_sq"), 1)
            dve.wait_ge(sem("qk_n"), 1)
            link(nc.vector.reciprocal(qkr[:, :, :], qkr[:, :, :]))
            newton(qkr[:, :, :], qkv2[:, :, :], nt[:, :].rearrange("p (n a) -> p n a", a=2))
            qkv = bk[:, 4:8, 0:384].rearrange("p k (n c) -> p k n c", n=2)

            def unit(dst, a):
                return nc.vector.tensor_tensor(dst.rearrange("p (k n) c -> p k n c", n=2), qkv[:, :, :, a * D:(a + 1) * D],
                                               wide(qkr[:, :, a].rearrange("p (k n) -> p k n", n=2), D), ALU.mult)

            unit(KK[:, :, 0:D], 1)
            unit(KK[:, :, D:2 * D], 1).then_inc(sem("KK"), 1)
            unit(QV[:, :, 0:D], 0).then_inc(sem("QV"), 1)
            dve.wait_ge(sem("ld_g"), 32)
            dve.wait_ge(sem("gS"), 2)
            link(nc.vector.tensor_reduce(gsum[:, :], gS[:, :].rearrange("p (s c) -> p s c", c=C), AX, ALU.add))
            nc.vector.tensor_scalar(glin[:, :], gsum[:, :], gaff[:, 0:1], gaff[:, 1:2], ALU.mult, ALU.add).then_inc(sem("glin"), 1)
            dve.wait_ge(sem("cleared"), 1)
            dve.wait_ge(sem("kkT_ps"), 1)
            nc.vector.tensor_copy(kk[:, 2:4, 0:S], bk[:, 1, :].rearrange("p (b s) -> p b s", b=2)).then_inc(sem("kkT_v"), 1)
            dve.wait_ge(sem("qvT_ps"), 1)
            nc.vector.tensor_copy(vT[:, 2:4, 0:S], bk[:, 5, :].rearrange("p (b s) -> p b s", b=2)).then_inc(sem("kkT_v"), 1)
            nc.vector.tensor_copy(qq[0:D, 512:1024], bk[0:D, 5, :]).then_inc(sem("qq"), 1)
            dve.wait_ge(sem("gate_ps"), 1)
            nc.vector.tensor_copy(gates[:, :, :, 0:T], bk[:, 2, 0:3 * B * T].rearrange("p (g b t) -> p g b t", g=3, b=B)).then_inc(sem("gates"), 1)
            dve.wait_ge(sem("gates"), 1)
            for b in range(B):
                r = slice(32 * b, 32 * b + 32)
                nc.vector.tensor_copy(lrtok[r, 0:T], gates[r, 2, b, 0:T]).then_inc(sem("gates"), 1)
            dve.wait_ge(sem("kkT_a"), 2)
            nc.vector.memset(bk[:, 1:4:2, 0:DE], 0.0)
            nc.vector.memset(bk[:, 2, 2 * C * B:512 - D], 0.0).then_inc(sem("ps_clear"), 1)
            nc.vector.memset(og[:, :], 0.0).then_inc(sem("p2_new"), 1)
            nc.vector.memset(a0x[:, :], 0.0).then_inc(sem("m_new"), 1)

            with nc.vector.Fori(0, T, MEM_UN) as i:
                for u in range(MEM_UN):
                    t1 = i + (u + 1)
                    kc, vc = kcur[u % 2], vcur[u % 2]
                    dve.wait_ge(sem("a0q"), t1)
                    nc.vector.scalar_tensor_tensor(a0u[:, :], a0q[:, :], 1.0 / KAPPA, bk[:, 1, 0:DE], ALU.add, ALU.mult).then_inc(sem("a0u"), 1)
                    nc.vector.scalar_tensor_tensor(a0y[:, :], a0q[:, :], 1.0 / (3 * KAPPA), bk[:, 1, 0:DE], ALU.add, ALU.mult)
                    dve.wait_ge(sem("h1_ps"), t1)
                    nc.vector.tensor_tensor(h1T[64:128, :, 0:C], bk[64:128, 2, 0:64].rearrange("p (b c) -> p b c", b=B),
                                            kc[64:128, :, 0:C], ALU.add).then_inc(sem("h1T"), 1)
                    dve.wait_ge(sem("h1T"), t1)
                    nc.vector.tensor_tensor(hv[64:128, :, :], h1T[64:128, :, 0:C], vc[64:128, :, :], ALU.subtract).then_inc(sem("hv"), 1)
                    dve.wait_ge(sem("a0tq"), t1)
                    nc.vector.scalar_tensor_tensor(a0y[:, :], a0s[:, :], -1.0, a0y[:, :], ALU.add, ALU.mult).then_inc(sem("a0z"), 1)
                    dve.wait_ge(sem("a0z"), t1)
                    nc.vector.scalar_tensor_tensor(a0x[:, :], a0y[:, :], -3 * KAPPA * RT2PI, a0t[:, :], ALU.mult, ALU.add)
                    dve.wait_ge(sem("a1q"), t1)
                    nc.vector.scalar_tensor_tensor(a1u[:, :], a1q[:, :], 1.0 / KAPPA, bk[:, 3, 0:DE], ALU.add, ALU.mult).then_inc(sem("a1u"), 1)
                    nc.vector.scalar_tensor_tensor(a1y[:, :], a1q[:, :], 1.0 / (3 * KAPPA), bk[:, 3, 0:DE], ALU.add, ALU.mult).then_inc(sem("a1y"), 1)
                    dve.wait_ge(sem("hv"), t1)
                    dve.wait_ge(sem("pred_ps"), t1)
                    nc.vector.tensor_tensor(dT[64:128, :, 0:C], bk[64:128, 2, 64:128].rearrange("p (b c) -> p b c", b=B),
                                            hv[64:128, :, :], ALU.add).then_inc(sem("dT"), 1)
                    dve.wait_ge(sem("a1y"), t1)
                    dve.wait_ge(sem("a1tq"), t1)
                    nc.vector.scalar_tensor_tensor(a1y[:, :], a1s[:, :], -1.0, a1y[:, :], ALU.add, ALU.mult).then_inc(sem("a1z"), 1)
                    dve.wait_ge(sem("a1z"), t1)
                    nc.vector.scalar_tensor_tensor(a1x[:, :], a1y[:, :], -3 * KAPPA * RT2PI, a1t[:, :], ALU.mult, ALU.add).then_inc(sem("a1x"), 1)
                    dve.wait_ge(sem("a1x"), t1)
                    dve.wait_ge(sem("dg1_ps"), t1)
                    nc.vector.scalar_tensor_tensor(da1tok[:, :], a1x[:, :], 1.0, bk[:, 2, 128:128 + DE], ALU.add, ALU.mult).then_inc(sem("da1tok"), 1)
                    dve.wait_ge(sem("dh1_ps"), t1)
                    nc.vector.tensor_tensor(dh1T[64:128, :, 0:C], bk[64:128, 2, 256:320].rearrange("p (b c) -> p b c", b=B),
                                            dT[64:128, :, 0:C], ALU.add).then_inc(sem("dh1T"), 1)
                    dve.wait_ge(sem("dg0_ps"), t1)
                    nc.vector.scalar_tensor_tensor(da0tok[:, :], a0x[:, :], 1.0, bk[:, 2, 320:320 + DE], ALU.add, ALU.mult).then_inc(sem("da0tok"), 1)
                    dve.wait_ge(sem("Q"), t1)
                    dve.wait_ge(sem("grads"), t1)
                    nc.vector.tensor_tensor(P[:, :, 0:DE], Q[:, :, 0:DE], bk[:, 4:8, 0:DE], ALU.add).then_inc(sem("p1_new"), 1)
                    nc.vector.tensor_tensor(P[:, :, DE:2 * DE], Q[:, :, DE:2 * DE], bk[:, 4:8, DE:2 * DE], ALU.add).then_inc(sem("p2_new"), 1)
                    nc.vector.tensor_tensor(M[:, :, :], Me[:, :, :], bk[:, 4:8, 0:2 * DE], ALU.add).then_inc(sem("m_new"), 1)

            dve.wait_ge(sem("m_new"), T + 1)
            link(nc.vector.tensor_tensor(FW2[:, :, :], P[:, 0:2, :], P[:, 2:4, :], ALU.add))
            link(nc.vector.tensor_tensor(FW[:, :], FW2[:, 0, :], FW2[:, 1, :], ALU.add))
            nc.vector.tensor_scalar(FW[:, :], FW[:, :], 1.0 / B, None, ALU.mult).then_inc(sem("FW"), 1)
            dve.wait_ge(sem("zeros"), 1)
            nc.vector.memset(x2A[D:D + 1, :], 1.0).then_inc(sem("x2A"), 1)
            dve.wait_ge(sem("ld_3"), 48)
            nc.vector.tensor_scalar(sc0[:, :, 1:D], mid(w3[:, 0:D - 1], NT), 1.0, None, ALU.add)
            for n in range(2):
                dve.wait_ge(sem("f_h1_ps"), n + 1)
                nc.vector.tensor_tensor(h1F[64:128, n * 512:(n + 1) * 512], bk[64:128, 4 + n, :], qq[0:D, n * 512:(n + 1) * 512],
                                        ALU.add).then_inc(sem("f_h1"), 1)
            for n in range(2):
                dve.wait_ge(sem("f_y"), n + 1)
                ins = nc.vector.tensor_tensor(xs[:, 4 * n:4 * n + 4, :], xs[:, 4 * n:4 * n + 4, :],
                                              bk[:, n, 0:4 * D].rearrange("p (n d) -> p n d", n=4), ALU.add)
                link(ins)

            link(norm(xs[:, :, :], XT[:, :, D:2 * D], 1e-5, None))
            link(nc.vector.tensor_tensor(st[:, :], sd[:, :], sd[:, :], ALU.mult))
            link(nc.vector.tensor_tensor(rs[:, :], mv[:, :, 1], st[:, :], ALU.mult))
            nc.vector.tensor_scalar(rs[:, :], rs[:, :], 1e-5, None, ALU.add).then_inc(sem("var"), 1)
            rstd()
            nc.vector.tensor_tensor(XT[:, :, 0:D], XT[:, :, D:2 * D], wide(sd[:, :], D), ALU.mult).then_inc(sem("XT"), 1)
            for n in range(2):
                dve.wait_ge(sem("XT_ps"), n + 1)
                nc.vector.tensor_copy(t1T[64:128, n * 512:(n + 1) * 512], bk[64:128, 2 + n, :]).then_inc(sem("t1T"), 1)
            dve.wait_ge(sem("logit_ps"), 1)
            link(nc.vector.tensor_tensor(L[:, :, :], bk[:, 0, 0:NT * E].rearrange("p (n e) -> p n e", n=NT), mid(br[:, :], NT), ALU.add))

            def first_max(src, m, pick):
                link(nc.vector.tensor_reduce(m[:, :], src[:, :, :], AX, ALU.max))
                link(nc.vector.tensor_tensor(eq[:, :, :], src[:, :, :], wide(m[:, :], E), ALU.is_equal))
                flat = "p n e -> p (n e)"
                link(nc.vector.tensor_tensor_scan(cum[:, :, :].rearrange(flat), notfirst[:, :], eq[:, :, :].rearrange(flat),
                                                  0.0, ALU.mult, ALU.add))
                link(nc.vector.scalar_tensor_tensor(pick[:, :, :], cum[:, :, :], 1.0, eq[:, :, :], ALU.is_equal, ALU.mult))

            first_max(L, m1, pick1)
            link(nc.vector.scalar_tensor_tensor(L2[:, :, :], pick1[:, :, :], -3.0e38, L[:, :, :], ALU.mult, ALU.add))
            first_max(L2, m2, pick2)
            nc.vector.tensor_tensor(md[:, :], m1[:, :], m2[:, :], ALU.subtract).then_inc(sem("md"), 1)
            dve.wait_ge(sem("p12"), 1)
            nc.vector.tensor_scalar(p2[:, :], p1[:, :], -0.5, 0.5, ALU.mult, ALU.add)
            link(nc.vector.tensor_scalar(p1[:, :], p1[:, :], 0.5, 0.5, ALU.mult, ALU.add))
            link(nc.vector.tensor_tensor(pick1[:, :, :], pick1[:, :, :], wide(p1[:, :], E), ALU.mult))
            link(nc.vector.tensor_tensor(pick2[:, :, :], pick2[:, :, :], wide(p2[:, :], E), ALU.mult))
            nc.vector.tensor_tensor(W8[:, :, :], pick1[:, :, :], pick2[:, :, :], ALU.add).then_inc(sem("W8"), 1)

            nc.vector.tensor_tensor(fold[:, :], ident[:, 0:D], ident[:, D:2 * D], ALU.add)
            link(nc.vector.tensor_tensor(pick3[:, :], ident[:, 0:E], ident[:, 32:32 + E], ALU.add))
            link(nc.vector.tensor_tensor(pick3[:, :], pick3[:, :], ident[:, 64:64 + E], ALU.add))
            nc.vector.tensor_copy(sel.rearrange("p (e m) -> p e m", e=E), wide(pick3[:, :], 128)).then_inc(sem("sel"), 1)
            nc.vector.memset(t3T[D:D + 1, :, :], 1.0).then_inc(sem("t3T"), 1)
            dve.wait_ge(sem("ld_l"), 32)
            nc.vector.memset(lvh[D:D + 1, :, :], 0.0)
            nc.vector.tensor_scalar(lvh[0:D, :, :], lv[:, :, :], 0.5, None, ALU.mult)
            dve.wait_ge(sem("ld_3"), 48)
            nc.vector.tensor_scalar(b3n[:, :], b3[:, :], -1.0, None, ALU.mult)
            dve.wait_ge(sem("zeros3"), 1)

            def split(n):
                cols = slice(n * 512, (n + 1) * 512)
                dve.wait_ge(sem("W8T"), n + 1)
                link(nc.vector.tensor_copy(W3[0:E, cols], W8T[:, cols]))
                link(nc.vector.tensor_tensor(rest[32:32 + E, cols], W8T[:, cols], W3[0:E, cols], ALU.subtract))
                link(nc.vector.tensor_copy(W3[32:32 + E, cols], rest[32:32 + E, cols]))
                nc.vector.tensor_tensor(W3[64:64 + E, cols], rest[32:32 + E, cols], W3[32:32 + E, cols],
                                        ALU.subtract).then_inc(sem("W3"), 1)

            split(0)

            def add_back(hf):
                dve.wait_ge(sem("back"), hf + 1)
                link(nc.vector.tensor_tensor(xs[:, 4 * hf:4 * hf + 4, :], xs[:, 4 * hf:4 * hf + 4, :],
                                             bk[:, 2 + hf, 0:4 * D].rearrange("p (n d) -> p n d", n=4), ALU.add))

            for g in range(2 * E):
                dve.wait_ge(sem("hT"), (g + 1) * HC)
                dve.wait_ge(sem("spread"), g + 1)
                nc.vector.tensor_tensor(hT[:, g % E, :, :], hT[:, g % E, :, :], mid(bk[:, g % 2, :], HC), ALU.mult).then_inc(sem("hw"), 1)
                if g == 1:
                    split(1)
                if g == E:
                    dve.wait_ge(sem("down"), E)
                    nc.vector.tensor_copy(yT[0][:, :], bk[:, 2, :]).then_inc(sem("yT"), 1)
            add_back(0)
            dve.wait_ge(sem("down"), 2 * E)
            nc.vector.tensor_copy(yT[1][:, :], bk[:, 3, :]).then_inc(sem("yT"), 1)
            add_back(1)

            norm(xs[:, :, :], xn[:, :, :], 1e-6, "ln")
            dve.wait_ge(sem("ln"), 2)
            nc.vector.tensor_tensor(xs[:, :, :], xs[:, :, :], xn[:, :, :], ALU.add)
            for k, (need, bank) in enumerate(((1, 0), (2, 0), (3, 1))):
                dve.wait_ge(sem("z_ps"), need)
                nc.vector.tensor_scalar(inner(zim[bank]), bk[:, bank, 0:S].rearrange("p (y x) -> p y x", x=W), cb2[:, 0:1], None,
                                        ALU.add).then_inc(sem("z"), 1)
            for g in range(2):
                dve.wait_ge(sem("A3_ps"), g + 1)
                for c in range(2):
                    ins = nc.vector.tensor_copy(A3[:, c::2, 32 * g:32 * g + 32],
                                                bk[:, 2 + g, c * 128:(c + 1) * 128].rearrange("p (q o) -> p q o", q=B))
                link(ins)
            link(nc.vector.tensor_tensor(prod[:, :, 1:D + 1], A3[:, :, :], mid(w3[:, :], NT), ALU.mult))
            link(nc.vector.tensor_reduce(st[:, :], prod[:, :, 1:D + 1], AX, ALU.add))
            link(nc.vector.tensor_scalar(prod[:, :, 0:1], wide(st[:, :], 1), -1.0, b3n[:, 0:1], ALU.mult, ALU.add))
            link(nc.vector.tensor_tensor_scan(scanned[:, :, :].rearrange("p n d -> p (n d)"), sc0[:, :, :].rearrange("p n d -> p (n d)"),
                                              prod[:, :, :].rearrange("p n d -> p (n d)"), 0.0, ALU.mult, ALU.subtract))
            link(nc.vector.tensor_tensor(xs[:, :, :], xs[:, :, :], scanned[:, :, 0:D], ALU.add))

            norm(xs[:, :, :], xn[:, :, :], 1e-5, "ln")
            for n in range(2):
                dve.wait_ge(sem("t3T_ps"), n + 1)
                for c in range(2):
                    ins = nc.vector.tensor_copy(
                        t3T[0:D, c * 128:(c + 1) * 128, 2 * n:2 * n + 2].rearrange("p s b -> p b s"),
                        bk[0:D, 4 + n, :].rearrange("p (b c s) -> p b c s", b=2, c=2)[:, :, c, :])
                ins.then_inc(sem("t3T"), 1)
            link(nc.vector.memset(bk[0:D, 6, 0:32], 0.0))
            nc.vector.memset(bk[0:D, 6, 2:3 * B:3], 1.0).then_inc(sem("rec_init"), 1)
            nc.vector.memset(og[:, :], 0.0).then_inc(sem("h_new"), 1)
            HU = LSTM_UN // 2
            flat3 = "p b k -> p (b k)"
            with nc.vector.Fori(0, S, LSTM_UN) as i:
                for u in range(LSTM_UN):
                    t1 = i + (u + 1)
                    c_t = cs[u % 2]
                    if u % HU == 0:
                        dve.wait_ge(sem("h_saved"), i + (u + 1))
                    dve.wait_ge(sem("in_gate"), t1)
                    nc.vector.tensor_tensor_scan(c_t[:, :, :].rearrange(flat3), bk[0:D, 6, 0:3 * B], gp[:, :, :].rearrange(flat3),
                                                 0.0, ALU.mult, ALU.add).then_inc(sem("c_new"), 1)
                    dve.wait_ge(sem("tanh_c"), t1)
                    nc.vector.scalar_tensor_tensor(hring[0:D, u, :], og[:, :], 1.0, bk[0:D, 6, 16:16 + B],
                                                   ALU.add, ALU.mult).then_inc(sem("h_new"), 1)
                    dve.wait_ge(sem("h_new"), i + (u + 2))
                    nc.vector.scalar_tensor_tensor(gp[:, :, 2], hring[0:D, u, :], 0.5, c_t[:, :, 2], ALU.mult, ALU.mult).then_inc(sem("hc"), 1)
                    dve.wait_ge(sem("hc"), t1)

            dve.wait_ge(sem("hs_ps"), 1)
            nc.vector.scalar_tensor_tensor(xs[:, :, :], bk[:, 7, :].rearrange("p (n d) -> p n d", n=NT), 0.5, xs[:, :, :],
                                           ALU.mult, ALU.add).then_inc(sem("x_done"), 1)


def layouts(a):
    f = np.float32
    x = np.asarray(a["x"], f)
    o = {"x": np.ascontiguousarray(x.reshape(NT, 128, D).transpose(1, 0, 2))}
    o["ident"] = np.eye(128, dtype=f)
    pad = ((0, 128 - D), (0, 0))
    o["wqkv"] = np.pad(np.concatenate([a["L0_conv_Wq"], a["L0_conv_Wk"], a["L0_conv_Wv"]], axis=1), pad)
    o["wgate"] = np.pad(np.stack([a["L0_conv_w_eta"], a["L0_conv_w_forget"], a["L0_conv_w_lr"]], axis=1), pad)
    lr = -0.1 * 2.0 / (C * D)
    o["gaff"] = np.array([[0.5 / C, 0.5], [-0.5 / C, 0.5], [lr * 0.5 / C, lr * 0.5]], f)
    o["gsel"] = np.repeat(np.eye(3, dtype=f)[:, :, None], 128, axis=2)
    o["memw"] = np.concatenate([np.concatenate([a["L0_conv_w1_0"], a["L0_conv_w1_1"]], axis=0),
                                a["L0_conv_w2_0"], a["L0_conv_w2_1"]], axis=1)
    o["wr"] = np.asarray(a["L0_ffn_Wr"])
    o["br"] = np.repeat(np.asarray(a["L0_ffn_br"])[None, :], 128, axis=0)
    o["lng"] = np.asarray(a["L0_ffn_ln_g"]).T
    o["lnb"] = np.concatenate([np.asarray(a["L0_ffn_ln_b"]).T, np.ones((1, E), f)], axis=0)
    o["w1"] = np.concatenate([np.asarray(a["L0_ffn_W1"]).transpose(1, 0, 2), np.asarray(a["L0_ffn_b1"])[None]], axis=0)
    o["w2"] = np.asarray(a["L0_ffn_W2"]).reshape(E, HC, 128, D).transpose(2, 0, 1, 3)
    o["b2"] = np.asarray(a["L0_ffn_b2"])
    nf = np.ones((128, NT, E), f)
    nf[:, :, 0] = 0.0
    o["notfirst"] = nf.reshape(128, NT * E)
    w1, b1 = np.asarray(a["L1_conv_w1"])[0, 0], np.asarray(a["L1_conv_b1"])[0, 0, 0]
    ps = np.zeros((4, D + 1, D + 1), f)
    for g in range(4):
        ps[g] = np.eye(D + 1, dtype=f)
        ps[g][:, 16 * g:16 * g + 16] = np.concatenate([w1, b1[None, :]], axis=0)
    o["c1p"] = ps.transpose(2, 0, 1)
    o["c1last"] = ps[3]
    w2 = np.asarray(a["L1_conv_w2"]).reshape(9, D, 16).transpose(1, 0, 2)
    cw = np.zeros((6, B, 32, 9, B, 2, 16), f)
    for q in range(B):
        lo, hi = w2[0:32], w2[32:64]
        cw[0, q, :, :, q, 0] = lo
        cw[0, q, 16:, :, q, 1] = lo[16:]
        cw[1, q, :, :, q, 0] = hi
        cw[1, q, :, :, q, 1] = hi
        cw[2, q, :16, :, q, 1] = lo[:16]
        cw[3, q, :, :, q, 0] = hi
        cw[3, q, 16:, :, q, 1] = hi[16:]
        cw[4, q, :, :, q, 0] = lo
        cw[4, q, :, :, q, 1] = lo
        cw[5, q, :16, :, q, 1] = hi[:16]
    o["cw"] = cw.reshape(6, 128, 9, 128).transpose(1, 0, 2, 3)
    o["cb2"] = np.tile(np.asarray(a["L1_conv_b2"]).reshape(16), 8)[:, None]
    o["w3"] = np.repeat(np.asarray(a["L1_conv_w3"]).reshape(1, D), 128, axis=0)
    o["b3"] = np.repeat(np.asarray(a["L1_conv_b3"]).reshape(1, 1), 128, axis=0)
    o["lu"] = np.stack([np.concatenate([a["L1_ffn_U_" + g], np.asarray(a["L1_ffn_b_" + g])[None]], axis=0) for g in "cio"], axis=1)
    o["lv"] = np.stack([np.asarray(a["L1_ffn_V_" + g]) for g in "cio"], axis=1)
    return {k: np.ascontiguousarray(v) for k, v in o.items()}


def kernel(**inputs):
    import concourse.bacc as _bacc
    from concourse.bass_utils import run_bass_kernel_spmd as _run

    nc = _bacc.Bacc("TRN2", target_bir_lowering=False, num_devices=1)
    arrays, aps = {}, {}
    for name, v in layouts(inputs).items():
        arrays[f"in_{name}"] = v
        aps[name] = nc.dram_tensor(f"in_{name}", v.shape, mybir.dt.from_np(v.dtype), kind="ExternalInput").ap()
    out = nc.dram_tensor("out", (128, NT, D), F32, kind="ExternalOutput").ap()
    build(nc, aps, out)
    r = _run(nc, [arrays], core_ids=[0])
    got = r.results[0]["out"]
    return np.ascontiguousarray(got.transpose(1, 0, 2)).reshape(B, T, C, D)
```
